# Optimizing a Trainium2 kernel written in Bass

```python
import numpy as np
import jax
import jax.numpy as jnp

def _softmax(x, axis=-1):
    return jax.nn.softmax(x, axis=axis)

def _gelu(x):
    return jax.nn.gelu(x, approximate=True)

def _silu(x):
    return jax.nn.silu(x)

def _sigmoid(x):
    return jax.nn.sigmoid(x)

def _layernorm(x, axis=-1, eps=1e-05):
    m = jnp.mean(x, axis=axis, keepdims=True)
    v = jnp.var(x, axis=axis, keepdims=True)
    return (x - m) / jnp.sqrt(v + eps)

def _scatter_add(tgt, idx, src, axis=0):
    return tgt.at[idx].add(src)

def _segment_sum(src, seg, n):
    return jax.ops.segment_sum(src, seg, n)
kernel_name = 'mk_flamingo_gated_d2_seqx_r8_01f360'

def setup_inputs(seed: int=0):
    np.random.seed(seed)
    _w = jnp.asarray

    def _rec_inputs():
        import jax
        import jax.numpy as jnp
        _rk = jax.random.key(seed)
        x = -0.0002928 + 1 * jax.random.normal(jax.random.fold_in(_rk, 1), (16, 128, 256), jnp.float32)
        _lenS = 128 - jax.random.randint(jax.random.fold_in(_rk, 7), (16,), 0, max(1, 128 // 4) + 1, jnp.int32)
        _lenS2 = 128 - jax.random.randint(jax.random.fold_in(_rk, 8), (16,), 0, max(1, 128 // 4) + 1, jnp.int32)
        _ctx_2048P = jax.random.normal(jax.random.fold_in(_rk, 11), (16, 16, 256), jnp.float32)
        _ctx_2048c = jax.random.dirichlet(jax.random.fold_in(_rk, 511), 0.3 * jnp.ones((16,), jnp.float32), (16, 128))
        _ctx_2048t = jnp.einsum('bsk,bkd->bsd', _ctx_2048c, _ctx_2048P)
        _ctx_2048t = _ctx_2048t * jax.lax.rsqrt(jnp.mean(jnp.square(_ctx_2048t)) + 1e-12) * 0.953939
        ctx_2048 = -1.39393e-06 + 0.999914 * (_ctx_2048t + 0.3 * jax.random.normal(jax.random.fold_in(_rk, 611), (16, 128, 256), jnp.float32))
        _validS = jnp.arange(128)[None, :] < _lenS[:, None]
        _validS2 = jnp.arange(128)[None, :] < _lenS2[:, None]
        _causal = jnp.tril(jnp.ones((128, 128), dtype=bool))
        mask_Bx1x2048_fk1 = jnp.where(jnp.ones((16, 1, 256), dtype=bool), 1.0, 0.0).astype(jnp.float32)
        _g = jax.random.normal(jax.random.fold_in(_rk, 9001), (2, 2), jnp.float32)
        _g = jnp.sign(_g) * jnp.maximum(jnp.abs(_g), 1.0) + (_g == 0) * 1.0
        g_xattn = _g[0]
        g_ffn = _g[1]
        return (x, ctx_2048, mask_Bx1x2048_fk1, g_xattn, g_ffn)
    x, ctx_2048, mask_Bx1x2048_fk1, g_xattn, g_ffn = _rec_inputs()

    def _L0_xattn_setup():
        import math
        import jax, jax.numpy as jnp
        import numpy as np
        SIZE = 128
        HEADS = 16
        HEAD_DIM = SIZE // HEADS
        B, T, S = (2, 256, 256)
        NEG = 1000000.0
        key = jax.random.key(seed)
        ks = jax.random.split(key, 10)
        target = jax.random.normal(ks[0], (B, SIZE, T), dtype=jnp.float32)
        source = jax.random.normal(ks[1], (B, SIZE, S), dtype=jnp.float32)
        target_mask = (jax.random.uniform(ks[2], (B, 1, T)) > 0.1).astype(jnp.float32)
        source_mask = (jax.random.uniform(ks[3], (B, 1, S)) > 0.1).astype(jnp.float32)
        scale = 1.0 / math.sqrt(SIZE)
        Wq = jax.random.normal(ks[4], (SIZE, SIZE), dtype=jnp.float32) * scale
        Wk = jax.random.normal(ks[5], (SIZE, SIZE), dtype=jnp.float32) * scale
        Wv = jax.random.normal(ks[6], (SIZE, SIZE), dtype=jnp.float32) * scale
        bq = jax.random.normal(ks[7], (SIZE,), dtype=jnp.float32) * 0.01
        bk = jax.random.normal(ks[8], (SIZE,), dtype=jnp.float32) * 0.01
        bv = jax.random.normal(ks[9], (SIZE,), dtype=jnp.float32) * 0.01
        return {'target': target, 'source': source, 'target_mask': target_mask, 'source_mask': source_mask, 'Wq': Wq, 'bq': bq, 'Wk': Wk, 'bk': bk, 'Wv': Wv, 'bv': bv}
    _L0_xattn_all = _L0_xattn_setup()
    _L0_xattn_in = {k: v for k, v in _L0_xattn_all.items() if k in ('Wq', 'bq', 'Wk', 'bk', 'Wv', 'bv')}
    del _L0_xattn_all

    def _L0_ffn_setup():
        import jax, jax.numpy as jnp
        import numpy as np
        B, L, D = (4, 512, 256)
        DF = 4 * D
        CAPACITY_RATIO = 0.5
        key = jax.random.key(seed)
        ks = jax.random.split(key, 4)
        s = 0.02
        return {'x': jax.random.normal(ks[0], (B, L, D), dtype=jnp.float32), 'w_r': jax.random.normal(ks[1], (D,), dtype=jnp.float32) * s, 'b_r': jnp.zeros((), dtype=jnp.float32), 'w1': jax.random.normal(ks[2], (D, DF), dtype=jnp.float32) * s, 'b1': jnp.zeros((DF,), dtype=jnp.float32), 'w2': jax.random.normal(ks[3], (DF, D), dtype=jnp.float32) * s, 'b2': jnp.zeros((D,), dtype=jnp.float32)}
    _L0_ffn_all = _L0_ffn_setup()
    _L0_ffn_in = {k: v for k, v in _L0_ffn_all.items() if k in ('w_r', 'b_r', 'w1', 'b1', 'w2', 'b2')}
    del _L0_ffn_all

    def _L1_xattn_setup():
        import jax, jax.numpy as jnp
        import numpy as np
        N_HEAD = 8
        key = jax.random.key(seed)
        k1, k2, k3 = jax.random.split(key, 3)
        B, D, L = (4, 128, 256)
        q = jax.random.normal(k1, (B, D, L), dtype=jnp.float32)
        k = jax.random.normal(k2, (B, D, L), dtype=jnp.float32)
        v = jax.random.normal(k3, (B, D, L), dtype=jnp.float32)
        gamma = jnp.ones((), dtype=jnp.float32)
        return {'q': q, 'k': k, 'v': v, 'gamma': gamma}
    _L1_xattn_all = _L1_xattn_setup()
    _L1_xattn_in = {k: v for k, v in _L1_xattn_all.items() if k in ('gamma',)}
    del _L1_xattn_all

    def _L1_ffn_setup():
        import jax, jax.numpy as jnp
        import numpy as np
        HIDDEN = 256
        INTER = 688
        LUT_SIZE = 16

        def _ghost_linear(x, idx, lut):
            w = lut[idx]
            return jnp.einsum('bsh,oh->bso', x, w)
        key = jax.random.key(seed)
        k_x, k_lut, k_g, k_u, k_d = jax.random.split(key, 5)
        x = jax.random.normal(k_x, (2, 512, HIDDEN), dtype=jnp.float32)
        lut = jax.random.normal(k_lut, (LUT_SIZE,), dtype=jnp.float32) * 0.02
        gate_idx = jax.random.randint(k_g, (INTER, HIDDEN), 0, LUT_SIZE, dtype=jnp.int32)
        up_idx = jax.random.randint(k_u, (INTER, HIDDEN), 0, LUT_SIZE, dtype=jnp.int32)
        down_idx = jax.random.randint(k_d, (HIDDEN, INTER), 0, LUT_SIZE, dtype=jnp.int32)
        return {'x': x, 'lut': lut, 'gate_idx': gate_idx, 'up_idx': up_idx, 'down_idx': down_idx}
    _L1_ffn_all = _L1_ffn_setup()
    _L1_ffn_in = {k: v for k, v in _L1_ffn_all.items() if k in ('lut', 'gate_idx', 'up_idx', 'down_idx')}
    del _L1_ffn_all
    return {'x': x, 'ctx_2048': ctx_2048, 'mask_Bx1x2048_fk1': mask_Bx1x2048_fk1, 'g_xattn': g_xattn, 'g_ffn': g_ffn, 'L0_xattn_Wq': _L0_xattn_in['Wq'], 'L0_xattn_bq': _L0_xattn_in['bq'], 'L0_xattn_Wk': _L0_xattn_in['Wk'], 'L0_xattn_bk': _L0_xattn_in['bk'], 'L0_xattn_Wv': _L0_xattn_in['Wv'], 'L0_xattn_bv': _L0_xattn_in['bv'], 'L0_ffn_w_r': _L0_ffn_in['w_r'], 'L0_ffn_b_r': _L0_ffn_in['b_r'], 'L0_ffn_w1': _L0_ffn_in['w1'], 'L0_ffn_b1': _L0_ffn_in['b1'], 'L0_ffn_w2': _L0_ffn_in['w2'], 'L0_ffn_b2': _L0_ffn_in['b2'], 'L1_xattn_gamma': _L1_xattn_in['gamma'], 'L1_ffn_lut': _L1_ffn_in['lut'], 'L1_ffn_gate_idx': _L1_ffn_in['gate_idx'], 'L1_ffn_up_idx': _L1_ffn_in['up_idx'], 'L1_ffn_down_idx': _L1_ffn_in['down_idx']}

def reference(x, ctx_2048, mask_Bx1x2048_fk1, g_xattn, g_ffn, L0_xattn_Wq, L0_xattn_bq, L0_xattn_Wk, L0_xattn_bk, L0_xattn_Wv, L0_xattn_bv, L0_ffn_w_r, L0_ffn_b_r, L0_ffn_w1, L0_ffn_b1, L0_ffn_w2, L0_ffn_b2, L1_xattn_gamma, L1_ffn_lut, L1_ffn_gate_idx, L1_ffn_up_idx, L1_ffn_down_idx):
    import jax
    import jax.numpy as jnp

    def _L0_xattn_ref(target, source, target_mask, source_mask, Wq, bq, Wk, bk, Wv, bv):
        import math
        import jax, jax.numpy as jnp
        import numpy as np
        SIZE = 128
        HEADS = 16
        HEAD_DIM = SIZE // HEADS
        B, T, S = (2, 256, 256)
        NEG = 1000000.0
        b, _, t = target.shape
        s = source.shape[-1]
        q = jnp.einsum('oc,bct->bot', Wq, target) + bq[None, :, None]
        k = jnp.einsum('oc,bcs->bos', Wk, source) + bk[None, :, None]
        v = jnp.einsum('oc,bcs->bos', Wv, source) + bv[None, :, None]
        q = q.reshape(b, HEADS, HEAD_DIM, t)
        k = k.reshape(b, HEADS, HEAD_DIM, s)
        v = v.reshape(b, HEADS, HEAD_DIM, s)
        dot = jnp.einsum('bhdt,bhds->bhts', q, k) / math.sqrt(HEAD_DIM)
        mask = target_mask[:, :, :, None] * source_mask[:, :, None, :]
        dot = mask * dot - (1.0 - mask) * NEG
        amap = jax.nn.softmax(dot, axis=-1) * mask
        out = jnp.einsum('bhts,bhds->bhdt', amap, v)
        return out.reshape(b, HEADS * HEAD_DIM, t)

    def _L0_ffn_ref(x, w_r, b_r, w1, b1, w2, b2):
        import jax, jax.numpy as jnp
        import numpy as np
        B, L, D = (4, 512, 256)
        DF = 4 * D
        CAPACITY_RATIO = 0.5
        b, l, d = x.shape
        k = int(l * CAPACITY_RATIO)
        scores = jnp.einsum('bld,d->bl', x, w_r) + b_r
        _, idx = jax.lax.top_k(scores, k)
        x_sel = jnp.take_along_axis(x, idx[:, :, None], axis=1)
        h = jax.nn.gelu(jnp.einsum('bkd,df->bkf', x_sel, w1) + b1)
        out_sel = jnp.einsum('bkf,fd->bkd', h, w2) + b2
        batch_ix = jnp.arange(b)[:, None]
        out = jnp.zeros_like(x).at[batch_ix, idx].set(out_sel)
        return out

    def _L1_xattn_ref(q, k, v, gamma):
        import jax, jax.numpy as jnp
        import numpy as np
        N_HEAD = 8
        B, Dq, Lq = q.shape
        Dv, Lk = (v.shape[-2], v.shape[-1])
        h = N_HEAD
        dq = Dq // h
        dv = Dv // h
        qh = q.reshape(B, h, dq, Lq)
        kh = k.reshape(B, h, dq, Lk)
        vh = v.reshape(B, h, dv, Lk)
        scale = 1.0 / jnp.sqrt(jnp.asarray(dq, dtype=q.dtype))
        qk = jnp.einsum('bhdq,bhdl->bhql', qh, kh) * scale
        sm = jax.nn.softmax(qk, axis=-1)
        ret = jnp.einsum('bhql,bhdl->bhdq', sm, vh)
        ret = ret.reshape(B, Dv, Lq)
        return gamma * ret

    def _L1_ffn_ref(x, lut, gate_idx, up_idx, down_idx):
        import jax, jax.numpy as jnp
        import numpy as np
        HIDDEN = 256
        INTER = 688
        LUT_SIZE = 16

        def _ghost_linear(x, idx, lut):
            w = lut[idx]
            return jnp.einsum('bsh,oh->bso', x, w)
        gate = _ghost_linear(x, gate_idx, lut)
        up = _ghost_linear(x, up_idx, lut)
        h = jax.nn.silu(gate) * up
        return _ghost_linear(h, down_idx, lut)
    x = x + jnp.tanh(g_xattn[0]) * _L0_xattn_ref(_layernorm(x, axis=-1), ctx_2048, mask_Bx1x2048_fk1, mask_Bx1x2048_fk1, L0_xattn_Wq, L0_xattn_bq, L0_xattn_Wk, L0_xattn_bk, L0_xattn_Wv, L0_xattn_bv)
    x = x + jnp.tanh(g_ffn[0]) * _L0_ffn_ref(_layernorm(x, axis=-1), L0_ffn_w_r, L0_ffn_b_r, L0_ffn_w1, L0_ffn_b1, L0_ffn_w2, L0_ffn_b2)
    x = x + jnp.tanh(g_xattn[1]) * _L1_xattn_ref(_layernorm(x, axis=-1), ctx_2048, ctx_2048, L1_xattn_gamma)
    x = x + jnp.tanh(g_ffn[1]) * _L1_ffn_ref(_layernorm(x, axis=-1), L1_ffn_lut, L1_ffn_gate_idx, L1_ffn_up_idx, L1_ffn_down_idx)
    return x

_drawn_inputs = setup_inputs


def setup_inputs(seed=0):
    import zlib

    import numpy as np

    out = dict(_drawn_inputs(seed))
    spreads = {'g_ffn': (-1.0, 0.6), 'L0_ffn_b1': (0.0, 0.548), 'L0_ffn_b2': (0.0, 0.1)}
    factors = {'L0_xattn_bq': 8.0, 'L0_xattn_bk': 8.0, 'L0_xattn_bv': 5.707}
    for name, (base, spread) in spreads.items():
        noise = np.random.default_rng([zlib.crc32(name.encode()), seed]).standard_normal(out[name].shape)
        drawn = base * np.exp(spread * noise) if base else spread * noise
        out[name] = jnp.asarray(drawn.astype(out[name].dtype))
    for name, factor in factors.items():
        out[name] = (out[name] * factor).astype(out[name].dtype)
    return out
```

```python
from contextlib import ExitStack

import numpy as np

import concourse.bass as bass
from concourse import mybir

F32 = mybir.dt.float32
F32R = mybir.dt.float32r
I32 = mybir.dt.int32
U32 = mybir.dt.uint32
ALU = mybir.AluOpType
ACT = mybir.ActivationFunctionType
AX = mybir.AxisListType

B, C, T = 16, 128, 256
NB = 2
NP = B // NB
N = NB * T
DF, FC = 1024, 8
INTER, OC = 688, 6
OM = [min(128, INTER - 128 * o) for o in range(OC)]
KEEP = 64
LUT = 16
EPS = 1e-5
NEG = 1e6
GELU_C = float(np.sqrt(2.0 / np.pi))


class Layer:

    def __init__(self, heads, masked):
        self.H = heads
        self.DH = 128 // heads
        self.HPG = 32 // self.DH
        self.NG = 4
        self.SHIFT = 98 if masked else 96
        self.KE = self.SHIFT + 2 * self.HPG
        self.U = heads * NB
        self.NT = heads // 4
        self.scale = 1.0 / float(np.sqrt(self.DH))


L0 = Layer(16, True)
L1 = Layer(8, False)
NEG0 = NEG / L0.scale
NEG_HI = float(np.round(NEG0 / 2048) * 2048)
NEG_LO = NEG0 - NEG_HI


def lim(count):
    return min(count, NP) if isinstance(count, int) else count


def due(count):
    return not isinstance(count, int) or count > 0


def settle(eng, passed, count=None):
    if not isinstance(count, int):
        eng.sem_inc(passed, 1)


def flamingo_kernel(nc, a, out):
    with ExitStack() as ctx:
        def sb(name, shape, dt=F32):
            return ctx.enter_context(nc.sbuf_tensor(name, shape, dt))

        def ps(name):
            return ctx.enter_context(nc.psum_tensor(name, [128, 512], F32))

        def sem(name):
            return ctx.enter_context(nc.semaphore(name))

        ident = sb("ident", [128, 128])
        tril = sb("tril", [128, 128])
        iota = sb("iota", [128, KEEP])
        wq, wk, wv = sb("wq", [128, 128]), sb("wk", [128, 128]), sb("wv", [128, 128])
        bqk = sb("bqk", [128, 2])
        bv = sb("bv", [128, 128])
        wr = sb("wr", [128, T])
        br = sb("br", [128, 1])
        w1 = sb("w1", [128, 2, DF])
        b1 = sb("b1", [128, FC])
        w2 = sb("w2", [128, FC, T])
        b2 = sb("b2", [128, T])
        wg = sb("wg", [128, 2, INTER])
        wu = sb("wu", [128, 2, INTER])
        wd = sb("wd", [128, OC, T])
        lut = sb("lut", [128, LUT], U32)
        lutx = sb("lutx", [128, LUT // 2], U32)
        gts = sb("gts", [128, 5])
        tg = sb("tg", [128, 4])
        tgx = sb("tgx", [128, 2])

        mhalf = sb("mhalf", [128, NB])
        xin, xr0, x1, x2, x3 = (sb(n, [128, NB, T]) for n in ("xin", "xr0", "x1", "x2", "x3"))
        ctx0, ctx1 = sb("ctx0", [128, NB, T]), sb("ctx1", [128, NB, T])
        xn0, xnf0, xn1, xnf1 = (sb(n, [128, NB, T]) for n in ("xn0", "xnf0", "xn1", "xnf1"))
        mrA, mrB = sb("mrA", [128, NB, T]), sb("mrB", [128, NB, T])
        mc = sb("mc", [128, NB * 2])
        stat = [sb(f"stat{i}", [128, NB, 6]) for i in range(4)]
        mv = [sb(f"mv{i}", [128, NB, 2]) for i in range(4)]
        rstd = [sb(f"rstd{i}", [128, NB]) for i in range(4)]

        qf = sb("qf", [128, N])
        kf = sb("kf", [128, N])
        vf = sb("vf", [128, N])
        qh, ql, kh, kl = (sb(n, [128, N], F32R) for n in ("qh", "ql", "kh", "kl"))
        mrows, srows = sb("mrows", [128, N]), sb("srows", [128, N])
        ngh = mrows[32:33, :].bitcast(F32R)
        ngl = mrows[64:65, :].bitcast(F32R)
        mt = mrows[96:98, :].bitcast(F32R)
        chi, clo = srows[0:L0.H, :].bitcast(F32R), srows[32:32 + L0.H, :].bitcast(F32R)
        ones = srows[64:66, :]
        QT = [sb(f"QT{i}", [128, L.NG, N], F32R) for i, L in enumerate((L0, L1))]
        KM = [sb(f"KM{i}", [128, L.H, N], F32R) for i, L in enumerate((L0, L1))]
        V = [sb(f"V{i}", [128, 2 * NB, L.H, 32]) for i, L in enumerate((L0, L1))]
        mx = sb("mx", [128, NB, 2, L0.H])
        PR = 8
        P = sb("P", [128, PR, 512])
        OG = sb("OG", [128, 2, 512])
        Oc, Dc = sb("Oc", [128, N]), sb("Dc", [128, N])

        rs = sb("rs", [128, NB, 4])
        prod = sb("prod", [128, T])
        sbc = sb("sbc", [128, NB, 128])
        oh = sb("oh", [128, NB, KEEP])
        ohT = sb("ohT", [128, 128])
        xsT = sb("xsT", [128, 2, 128])
        z = sb("z", [128, DF])
        gz = sb("gz", [128, DF])
        y0 = sb("y0", [128, T])

        arena = sb("arena", [128, 2816])
        h1 = arena[:, 0:1536].rearrange("p (o n) -> p o n", o=OC)
        xT = arena[:, 1536:2048].rearrange("p (d n) -> p d n", d=2)
        th = arena[:, 2048:2560].rearrange("p (k n) -> p k n", k=2)
        ga1 = arena[:, 2560:2816]
        CH = 384
        lk = [arena[:, CH * j:CH * (j + 1)].bitcast(U32) for j in range(7)]

        mxp = [ps("mxp0"), ps("mxp1")]
        exq = [ps("exq0"), ps("exq1"), ps("exq2")]
        pv = ps("pv")
        pa = ps("pa")
        pf = ps("pf")

        ld_w, ld_b, ld_m, ld_i = sem("ld_w"), sem("ld_b"), sem("ld_m"), sem("ld_i")
        ld_in, ld_c1, ld_mb = sem("ld_in"), sem("ld_c1"), sem("ld_mb")
        set_z, set_o = sem("set_z"), sem("set_o")
        s_tg = sem("s_tg")
        lku = sem("lku")
        ln = [sem(f"ln{i}") for i in range(4)]
        xcp = sem("xcp")
        s_qp, s_qf, s_kp, s_kf, s_vp, s_vf = (sem(n) for n in ("s_qp", "s_qf", "s_kp", "s_kf", "s_vp", "s_vf"))
        pl0, pl1, pm, plv = sem("pl0"), sem("pl1"), sem("pm"), sem("plv")
        v1p, v1c = sem("v1p"), sem("v1c")
        asm = [sem("asm0"), sem("asm1")]
        mp, md = [sem("mp0"), sem("mp1")], [sem("md0"), sem("md1")]
        cp, ch, cl, cd = ([sem(f"{n}{i}") for i in range(2)] for n in ("cp", "ch", "cl", "cd"))
        sc, ex, pvd, og = ([sem(f"{n}{i}") for i in range(2)] for n in ("sc", "ex", "pvd", "og"))
        oc = [[sem(f"oc{i}{j}") for j in range(2)] for i in range(2)]
        rc, dv, om, xo = ([sem(f"{n}{i}") for i in range(2)] for n in ("rc", "dv", "om", "xo"))
        rt, rtp, rr, set_v = sem("rt"), sem("rtp"), sem("rr"), sem("set_v")
        xsp, xsc, hp, hz = sem("xsp"), sem("xsc"), sem("hp"), sem("hz")
        g_sq, g_in, g_th, g_h = sem("g_sq"), sem("g_in"), sem("g_th"), sem("g_h")
        yp, yc, x2q, x2p, x2c = (sem(n) for n in ("yp", "yc", "x2q", "x2p", "x2c"))
        xtp, xtc, gup, s_th, s_ga, s_h1 = (sem(n) for n in ("xtp", "xtc", "gup", "s_th", "s_ga", "s_h1"))
        passed_sp, passed_dve, passed_pool = sem("passed_sp"), sem("passed_dve"), sem("passed_pool")
        dnp, x4c, stored = sem("dnp"), sem("x4c"), sem("stored")

        NASM = [3 * L0.NG + 3 * L0.H + 3, 3 * L1.NG + 3 * L1.H]
        NCD = [2 * L0.H, 2 * L1.H]

        def f32(ap):
            return ap.bitcast(F32)

        block = ctx.enter_context(nc.Block())


        def unit(k):
            return 4 * (k // 8) + k % 4, k // 4 % 2

        LKC = 19
        LKN = LKC * 12

        def lookup_chunk(c):
            if c < 8:
                w = (wg, wu)[c // 4]
                return w[:, :, :].rearrange("p d n -> p (d n)"), (c % 4) * 344, 344
            return wd[:, :, :].rearrange("p o n -> p (o n)"), (c - 8) * 384, 384

        def steps(i, m0=True, e0=True, f0=True, m1=True, f1=True):
            q, r, nx = i - 1, i - 2, i + 1
            if m0:
                yield "load", nx, 0
            if m1:
                yield "norm1", q, 0
                yield "split1", q, 0
                yield "assemble1", q, 0
            if f1:
                yield "norm3", r, 0
                yield "turn3", r, 0
                yield "up3", r, 0
            if m1:
                yield "values1", q, 0
            if f1:
                yield "up3", r, 1
            lut_at = {} if f1 else {0: {8: 2, 20: 3}, 1: {8: 6, 20: 7}, -1: {0: 0}}.get(i, {})
            lut_at2 = {} if f1 else {0: {10: 4, 24: 5}, 1: {4: 8, 10: 9, 17: 10, 24: 11}, -1: {0: 1}}.get(i, {})
            for n in range(L0.U):
                if n in lut_at:
                    yield "lookup", 0, lut_at[n]
                if m0 and n == 4:
                    yield "norm0", nx, 0
                    yield "project0", nx, 0
                if e0:
                    yield "exp0", i, n
                if e0 and n % 4 == 2 and n >= 6:
                    yield "pv0", i, (n - 6) // 4
                    if n % 8 == 6 and n >= 14:
                        yield "out0", i, (n - 14) // 8
                if f1 and n % 6 == 3 and n < 24:
                    yield "up3", r, 2 + n // 6
                if m1 and 12 <= n < 28:
                    yield "max1", q, n - 12
                if f1 and n == 28:
                    yield "down3", r, 0
                if m1 and n == 28:
                    yield "shift1", q, 0
            if e0:
                yield "pv0", i, L0.U // 4 - 1
                yield "out0", i, L0.NT - 1
            if m0:
                yield "assemble0", nx, 0
                yield "values0", nx, 0
            for n in range(6):
                if m1:
                    yield "exp1", q, n
            for n in range(L0.U):
                if n in lut_at2:
                    yield "lookup", 0, lut_at2[n]
                if n == 1 and e0:
                    yield "resid0", i, 0
                if n == 1 and m0:
                    yield "keep0", nx, 0
                if n == 1 and f0:
                    yield "route", i, 0
                if m0:
                    yield "max0", nx, n
                if m1 and n % 3 == 0 and n < 30:
                    u = 6 + n // 3
                    yield "exp1", q, u
                    if u % 4 == 2:
                        yield "pv1", q, (u - 6) // 4
                        if u == 14:
                            yield "out1", q, 0
                if f0:
                    if n == 5:
                        yield "rank", i, 0
                    if n == 9:
                        yield "pick", i, 0
                    if n in (12, 14):
                        yield "up2", i, (n - 12) // 2
                    if n == 15:
                        yield "gelu", i, 0
                    if n == 24:
                        yield "down2", i, 0
                    if n == 27:
                        yield "spread", i, 0
                if n == 28 and m1:
                    yield "pv1", q, L1.U // 4 - 1
                    yield "out1", q, 1
            if m0:
                yield "shift0", nx, 0
            if m1:
                yield "resid1", q, 0
            if f0:
                yield "add2", i, 0

        def program(eng, step):
            for i in (-1, 0, 1, 2):
                for name, p, k in steps(i, m0=True, e0=i >= 0, f0=i >= 0, m1=i >= 1, f1=i >= 2):
                    step(name, p, k)
            with eng.Fori(3, NP - 1) as i:
                for name, p, k in steps(i):
                    step(name, p, k)
            for i in (NP - 1, NP, NP + 1):
                for name, p, k in steps(i, m0=False, e0=i < NP, f0=i < NP, m1=i <= NP, f1=True):
                    step(name, p, k)

        def layer(name):
            i = int(name[-1])
            return i, (L0, L1)[i]

        @block.sync
        def _(sp):
            def rows(ap):
                return ap.rearrange("(a d) -> a d", a=1)

            def inputs0(p):
                if due(p):
                    sp.wait_ge(xcp, p)
                settle(sp, passed_sp, p)
                if due(p):
                    sp.wait_ge(s_vp, p)
                settle(sp, passed_sp, p)
                if due(p):
                    sp.wait_ge(plv, p)
                settle(sp, passed_sp, p)
                if due(3 * p):
                    sp.wait_ge(pm, 3 * p)
                settle(sp, passed_sp, 3 * p)
                if due(6 * p):
                    sp.wait_ge(pl0, 6 * p)
                settle(sp, passed_sp, 6 * p)
                pair = bass.ds(p * NB, NB)
                sp.dma_start(xin[:, :, :], a["x"][pair].rearrange("b c t -> c b t")).then_inc(ld_in, 16)
                sp.dma_start(ctx0[:, :, :], a["ctx_2048"][pair].rearrange("b c t -> c b t")).then_inc(ld_in, 16)
                sp.dma_start(mrA[:, :, :].rearrange("p b t -> p (b t)"),
                             a["mrow"][bass.ds(p, 1), :].to_broadcast([128, N])).then_inc(ld_in, 16)
                sp.dma_start(mc[:, :], a["mcol"][bass.ds(p, 1)].rearrange("a p k -> (a p) k")).then_inc(ld_in, 16)

            def context1(p):
                if due(4 * p):
                    sp.wait_ge(pl1, 4 * p)
                settle(sp, passed_sp, 4 * p)
                if due(p):
                    sp.wait_ge(v1p, p)
                settle(sp, passed_sp, p)
                sp.dma_start(ctx1[:, :, :], a["ctx_2048"][bass.ds(p * NB, NB)].rearrange("b c t -> c b t")).then_inc(ld_c1, 16)

            def target_mask(p):
                if due(p):
                    sp.wait_ge(om[0], p)
                settle(sp, passed_sp, p)
                sp.dma_start(mrB[:, :, :].rearrange("p b t -> p (b t)"),
                             a["mrow"][bass.ds(p, 1), :].to_broadcast([128, N])).then_inc(ld_mb, 16)

            for dst, src in ((ident, a["ident"]), (wq, a["wqT"]), (wk, a["wkT"]), (wv, a["wvT"]), (bqk, a["bqk"])):
                sp.dma_start(dst[:, :], src).then_inc(ld_w, 16)
            sp.dma_start(bv[:, :], rows(a["L0_xattn_bv"]).to_broadcast([128, 128])).then_inc(ld_w, 16)
            sp.dma_start(gts[:, :], a["gts"].to_broadcast([128, 5])).then_inc(ld_w, 16)
            sp.dma_start(tril[:, :], a["tril"]).then_inc(ld_b, 16)
            sp.dma_start(iota[:, :], a["iota"].to_broadcast([128, KEEP])).then_inc(ld_b, 16)
            sp.dma_start(wr[:, :], rows(a["L0_ffn_w_r"]).to_broadcast([128, T])).then_inc(ld_b, 16)
            sp.dma_start(br[:, :], a["br"].to_broadcast([128, 1])).then_inc(ld_b, 16)
            sp.dma_start(lut[:, :], rows(a["L1_ffn_lut"]).to_broadcast([128, LUT]).bitcast(U32)).then_inc(ld_b, 16)
            sp.dma_start(wg[:, :, :].bitcast(I32), a["gate_i"]).then_inc(ld_i, 16)
            sp.dma_start(wu[:, :, :].bitcast(I32), a["up_i"]).then_inc(ld_i, 16)
            sp.dma_start(wd[:, :, :].bitcast(I32), a["down_i"]).then_inc(ld_i, 16)
            sp.wait_ge(set_z, 5)
            for L, km in ((L0, KM[0]), (L1, KM[1])):
                for h in range(L.H):
                    r = L.SHIFT + 2 * (h % L.HPG)
                    sp.dma_start(f32(km[r:r + 2, h, :]), ones[:, :]).then_inc(set_o, 16)
            sp.dma_start(w1[:, :, :], a["L0_ffn_w1"].rearrange("(k p) n -> p k n", p=128)).then_inc(ld_m, 16)
            sp.dma_start(b1[:, :], a["b1c"]).then_inc(ld_m, 16)
            sp.dma_start(w2[:, :, :], a["L0_ffn_w2"].rearrange("(k p) n -> p k n", p=128)).then_inc(ld_m, 16)
            sp.dma_start(b2[:, :], rows(a["L0_ffn_b2"]).to_broadcast([128, T])).then_inc(ld_m, 16)

            def step(name, p, k):
                if name in ("assemble0", "assemble1"):
                    i, L = layer(name)
                    if due((6, 4)[i] * (p + 1)):
                        sp.wait_ge((pl0, pl1)[i], (6, 4)[i] * (p + 1))
                    settle(sp, passed_sp, (6, 4)[i] * (p + 1))
                    if due(L.U * p):
                        sp.wait_ge(sc[i], L.U * p)
                    settle(sp, passed_sp, L.U * p)
                    for j, src in enumerate((qh, qh, ql)):
                        for G in range(L.NG):
                            sp.dma_start(f32(QT[i][32 * j:32 * j + 32, G, :]),
                                         f32(src[32 * G:32 * G + 32, :])).then_inc(asm[i], 16)
                    for j, src in enumerate((kh, kl, kh)):
                        for h in range(L.H):
                            r = 32 * j + L.DH * (h % L.HPG)
                            sp.dma_start(f32(KM[i][r:r + L.DH, h, :]),
                                         f32(src[L.DH * h:L.DH * h + L.DH, :])).then_inc(asm[i], 16)
                    if i == 0:
                        if due(3 * (p + 1)):
                            sp.wait_ge(pm, 3 * (p + 1))
                        settle(sp, passed_sp, 3 * (p + 1))
                        sp.dma_start(f32(QT[0][96:98, :, :]),
                                     f32(mt[:, :]).unsqueeze(1).to_broadcast([2, L.NG, N])).then_inc(asm[0], 16)
                        for j, src in enumerate((ngh, ngl)):
                            sp.dma_start(f32(KM[0][96 + j:97 + j, :, :]),
                                         f32(src[:, :]).unsqueeze(1).to_broadcast([1, L.H, N])).then_inc(asm[0], 16)
                elif name in ("shift0", "shift1"):
                    i, L = layer(name)
                    if due(p + 1):
                        sp.wait_ge(cl[i], p + 1)
                    settle(sp, passed_sp, p + 1)
                    for j, src in enumerate((chi, clo)):
                        for h in range(L.H):
                            r = L.SHIFT + 2 * (h % L.HPG) + j
                            sp.dma_start(f32(QT[i][r:r + 1, h // L.HPG, :]), f32(src[h:h + 1, :])).then_inc(cd[i], 16)
                elif name in ("out0", "out1"):
                    i, L = layer(name)
                    if due(L.NT * p + k + 1):
                        sp.wait_ge(og[i], L.NT * p + k + 1)
                    settle(sp, passed_sp, L.NT * p + k + 1)
                    if k == 0 and i == 0:
                        if due(p - 1):
                            sp.wait_ge(xo[1], p - 1)
                        settle(sp, passed_sp, p - 1)
                        if due(p):
                            sp.wait_ge(xo[0], p)
                        settle(sp, passed_sp, p)
                    if k == 0 and i == 1:
                        if due(lim(p + 2)):
                            sp.wait_ge(xo[0], lim(p + 2))
                        settle(sp, passed_sp, lim(p + 2))
                    for g in range(4):
                        r = L.DH * (4 * k + g)
                        for dst, q in ((Oc, 0), (Dc, L.DH)):
                            sp.dma_start(dst[r:r + L.DH, :],
                                         OG[32 * g + q:32 * g + q + L.DH, k % 2, :]).then_inc(oc[i][k % 2], 16)
                elif name == "load":
                    inputs0(p)
                elif name == "keep0":
                    target_mask(p)
                elif name == "route":
                    context1(p)
                elif name == "down3":
                    if due(p + 1):
                        sp.wait_ge(x4c, p + 1)
                    settle(sp, passed_sp, p + 1)
                    sp.dma_start(out[bass.ds(p * NB, NB)].rearrange("b c t -> c b t"), xnf1[:, :, :]).then_inc(stored, 16)

            program(sp, step)
            sp.wait_ge(stored, 16 * NP)

        @block.tensor
        def _(pe):
            def mm(o, l, r, start=True, stop=True):
                return nc.tensor.matmul(o, l, r, start=start, stop=stop, skip_group_check=True)

            def step(name, p, k):
                if name == "project0":
                    pe.wait_ge(ld_w, 16 * 7)
                    if due(8 * (p + 1)):
                        pe.wait_ge(ln[0], 8 * (p + 1))
                    if due(p - 1):
                        pe.wait_ge(v1c, p - 1)
                    if due(p):
                        pe.wait_ge(cl[0], p)
                    mm(pa[:, :], wq[:, :], xn0[:, :, :].rearrange("p b t -> p (b t)")).then_inc(s_qp, 1)
                    if due(64 * (p + 1)):
                        pe.wait_ge(ld_in, 64 * (p + 1))
                    if due(p + 1):
                        pe.wait_ge(s_qf, p + 1)
                    mm(pa[:, :], wk[:, :], ctx0[:, :, :].rearrange("p b t -> p (b t)")).then_inc(s_kp, 1)
                    if due(p + 1):
                        pe.wait_ge(s_kf, p + 1)
                    for b in range(NB):
                        for s in range(2):
                            j = 2 * b + s
                            last = mm(pa[:, 128 * j:128 * j + 128], ctx0[:, b, 128 * s:128 * s + 128], wv[:, :])
                    last.then_inc(s_vp, 1)
                elif name == "values1":
                    if due(16 * (p + 1)):
                        pe.wait_ge(ld_c1, 16 * (p + 1))
                    if due(lim(p + 2)):
                        pe.wait_ge(cl[0], lim(p + 2))
                    for b in range(NB):
                        for s in range(2):
                            j = 2 * b + s
                            last = nc.tensor.transpose(pa[:, 128 * j:128 * j + 128],
                                                       ctx1[:, b, 128 * s:128 * s + 128], ident[:, :])
                    last.then_inc(v1p, 1)
                elif name in ("max0", "max1"):
                    i, L = layer(name)
                    if k == 0:
                        if due(16 * NASM[i] * (p + 1)):
                            pe.wait_ge(asm[i], 16 * NASM[i] * (p + 1))
                        pe.wait_ge(set_o, 16 * (L0.H + L1.H))
                        if i == 0:
                            if due(L1.U * (p - 1)):
                                pe.wait_ge(md[1], L1.U * (p - 1))
                            if due(L0.U * p):
                                pe.wait_ge(md[0], L0.U * p)
                        else:
                            if due(L0.U * lim(p + 2)):
                                pe.wait_ge(md[0], L0.U * lim(p + 2))
                    elif k >= 2:
                        if due(L.U * p + k - 1):
                            pe.wait_ge(md[i], L.U * p + k - 1)
                    h, b = k // 2, k % 2
                    for s in range(2):
                        q0 = b * T + 128 * s
                        last = mm(mxp[k % 2][:, T * s:T * s + T], QT[i][0:L.SHIFT, h // L.HPG, q0:q0 + 128],
                                  KM[i][0:L.SHIFT, h, b * T:b * T + T])
                    last.then_inc(mp[i], 1)
                elif name in ("shift0", "shift1"):
                    i, L = layer(name)
                    if due(L.U * (p + 1)):
                        pe.wait_ge(md[i], L.U * (p + 1))
                    if i == 0:
                        if due(p - 1):
                            pe.wait_ge(cl[1], p - 1)
                        if due(p + 1):
                            pe.wait_ge(s_vf, p + 1)
                    else:
                        if due(lim(p + 3)):
                            pe.wait_ge(s_vf, lim(p + 3))
                        if due(p + 1):
                            pe.wait_ge(v1c, p + 1)
                    for b in range(NB):
                        for s in range(2):
                            j = 2 * b + s
                            last = mm(pa[0:L.H, 128 * j:128 * j + 128], mx[:, b, s, 0:L.H], ident[:, :])
                    last.then_inc(cp[i], 1)
                elif name in ("exp0", "exp1"):
                    i, L = layer(name)
                    if k == 0:
                        if due(16 * NCD[i] * (p + 1)):
                            pe.wait_ge(cd[i], 16 * NCD[i] * (p + 1))
                        if i == 0:
                            if due(L1.U * (p - 1)):
                                pe.wait_ge(ex[1], L1.U * (p - 1))
                            if due(L0.U * p):
                                pe.wait_ge(ex[0], L0.U * p)
                        else:
                            if due(L0.U * lim(p + 2)):
                                pe.wait_ge(ex[0], L0.U * lim(p + 2))
                    if k >= 3:
                        if due(L.U * p + k - 2):
                            pe.wait_ge(ex[i], L.U * p + k - 2)
                    h, b = unit(k)
                    for s in range(2):
                        k0 = b * T + 128 * s
                        last = mm(exq[(k + 2 * i) % 3][:, T * s:T * s + T], KM[i][0:L.KE, h, k0:k0 + 128],
                                  QT[i][0:L.KE, h // L.HPG, b * T:b * T + T])
                    last.then_inc(sc[i], 1)
                elif name in ("pv0", "pv1"):
                    i, L = layer(name)
                    if due(L.U * p + 4 * k + 4):
                        pe.wait_ge(ex[i], L.U * p + 4 * k + 4)
                    if k == 0:
                        if due(p + 1):
                            pe.wait_ge((plv, v1c)[i], p + 1)
                        if i == 0:
                            if due(L1.NT * (p - 1)):
                                pe.wait_ge(og[1], L1.NT * (p - 1))
                            if due(L0.NT * p):
                                pe.wait_ge(og[0], L0.NT * p)
                        else:
                            if due(L0.NT * lim(p + 2)):
                                pe.wait_ge(og[0], L0.NT * lim(p + 2))
                    elif k % 2 == 0:
                        if due(L.NT * p + k // 2):
                            pe.wait_ge(og[i], L.NT * p + k // 2)
                    b = k % 2
                    for s in range(2):
                        for g in range(4):
                            h = 4 * (k // 2) + g
                            last = mm(pv[32 * g:32 * g + 32, b * T:b * T + T], V[i][:, 2 * b + s, h, :],
                                      P[:, (4 * k + g) % PR, T * s:T * s + T], start=s == 0, stop=s == 1)
                    last.then_inc(pvd[i], 1)
                elif name == "rank":
                    if due(12 * p + 6):
                        pe.wait_ge(rt, 12 * p + 6)
                    if due(p - 1):
                        pe.wait_ge(x4c, p - 1)
                    if due(p):
                        pe.wait_ge(x2c, p)
                    for b in range(NB):
                        last = nc.tensor.transpose(pf[:, 128 * b:128 * b + 128], sbc[:, b, :], ident[:, :])
                    last.then_inc(rtp, 1)
                elif name == "pick":
                    if due(12 * p + 12):
                        pe.wait_ge(rt, 12 * p + 12)
                    for d in range(2):
                        for b in range(NB):
                            o = 128 * d + KEEP * b
                            mm(pf[:, o:o + KEEP], xnf0[:, b, 128 * d:128 * d + 128], oh[:, b, :])
                    nc.tensor.transpose(pf[:, 256:384], oh[:, :, :].rearrange("p b k -> p (b k)"), ident[:, :]).then_inc(xsp, 1)
                elif name == "up2":
                    if k == 0:
                        pe.wait_ge(ld_m, 16 * 4)
                        if due(2 * (p + 1)):
                            pe.wait_ge(xsc, 2 * (p + 1))
                    else:
                        if due(2 * p + 1):
                            pe.wait_ge(hz, 2 * p + 1)
                    for f in range(4):
                        for d in range(2):
                            c0 = 128 * (4 * k + f)
                            last = mm(pf[:, 128 * f:128 * f + 128], w1[:, d, c0:c0 + 128], xsT[:, d, :],
                                      start=d == 0, stop=d == 1)
                    last.then_inc(hp, 1)
                elif name == "down2":
                    if due(p + 1):
                        pe.wait_ge(g_h, p + 1)
                    for f in range(FC):
                        last = mm(pf[:, 0:T], z[:, 128 * f:128 * f + 128], w2[:, f, :], start=f == 0, stop=f == FC - 1)
                    last.then_inc(yp, 1)
                elif name == "spread":
                    if due(p + 1):
                        pe.wait_ge(yc, p + 1)
                    mm(pf[:, 0:T], ohT[0:KEEP, :], y0[0:KEEP, :]).then_inc(x2q, 1)
                    if due(p + 1):
                        pe.wait_ge(x2q, p + 1)
                    mm(pf[:, T:2 * T], ohT[KEEP:2 * KEEP, :], y0[KEEP:2 * KEEP, :]).then_inc(x2p, 1)
                elif name == "turn3":
                    if due(8 * (p + 1)):
                        pe.wait_ge(ln[3], 8 * (p + 1))
                    if due(lim(p + 2)):
                        pe.wait_ge(x2c, lim(p + 2))
                    for d in range(2):
                        for b in range(NB):
                            o = T * d + 128 * b
                            last = nc.tensor.transpose(pf[:, o:o + 128], xnf1[:, b, 128 * d:128 * d + 128], ident[:, :])
                    last.then_inc(xtp, 1)
                elif name == "up3":
                    if k == 0:
                        if due(p + 1):
                            pe.wait_ge(xtc, p + 1)
                        pe.wait_ge(lku, LKN)
                    else:
                        if due(OC * p + k):
                            pe.wait_ge(s_h1, OC * p + k)
                    for w, o in ((wg, 0), (wu, T)):
                        for d in range(2):
                            last = mm(pf[0:OM[k], o:o + T], w[:, d, 128 * k:128 * k + OM[k]], xT[:, d, :],
                                      start=d == 0, stop=d == 1)
                    last.then_inc(gup, 1)
                elif name == "down3":
                    if due(OC * (p + 1)):
                        pe.wait_ge(s_h1, OC * (p + 1))
                    for b in range(NB):
                        for o in range(OC):
                            last = mm(pf[:, T * b:T * b + T], h1[0:OM[o], o, 128 * b:128 * b + 128],
                                      wd[0:OM[o], o, :], start=o == 0, stop=o == OC - 1)
                    last.then_inc(dnp, 1)

            program(pe, step)

        @block.scalar
        def _(act):
            act.wait_ge(ld_w, 16 * 7)
            nc.scalar.activation(tg[:, :], gts[:, 0:4], ACT.Tanh).then_inc(s_tg, 1)

            def step(name, p, k):
                if name == "project0":
                    for dst, bank, prod_, done, j in ((qf, pa, s_qp, s_qf, 0), (kf, pa, s_kp, s_kf, 1)):
                        if due(p + 1):
                            act.wait_ge(prod_, p + 1)
                        if due(6 * p):
                            act.wait_ge(pl0, 6 * p)
                        nc.scalar.activation(dst[:, :], bank[:, :], ACT.Identity, bias=bqk[:, j:j + 1]).then_inc(done, 1)
                elif name == "values1":
                    if due(p + 1):
                        act.wait_ge(v1p, p + 1)
                    if due(L1.U // 4 * p):
                        act.wait_ge(pvd[1], L1.U // 4 * p)
                    act.wait_ge(set_z, 5)
                    nc.scalar.copy(V[1][:, :, :, 0:L1.DH],
                                   pa[:, :].rearrange("p (j h d) -> p j h d", j=4, h=L1.H)).then_inc(v1c, 1)
                elif name in ("shift0", "shift1"):
                    i, L = layer(name)
                    if due(p + 1):
                        act.wait_ge(cp[i], p + 1)
                    if i == 0:
                        if due(16 * NCD[1] * (p - 1)):
                            act.wait_ge(cd[1], 16 * NCD[1] * (p - 1))
                        if due(16 * NCD[0] * p):
                            act.wait_ge(cd[0], 16 * NCD[0] * p)
                    else:
                        if due(16 * NCD[0] * lim(p + 2)):
                            act.wait_ge(cd[0], 16 * NCD[0] * lim(p + 2))
                    nc.scalar.activation(chi[0:L.H, :], pa[0:L.H, :], ACT.Copy, scale=-1.0).then_inc(ch[i], 1)
                elif name in ("exp0", "exp1"):
                    i, L = layer(name)
                    if due(L.U * p + k + 1):
                        act.wait_ge(sc[i], L.U * p + k + 1)
                    if k % 4 == 0:
                        if k >= PR:
                            if due(L.U // 4 * p + (k - PR) // 4 + 1):
                                act.wait_ge(pvd[i], L.U // 4 * p + (k - PR) // 4 + 1)
                        elif i == 0:
                            if due(L1.U // 4 * (p - 1)):
                                act.wait_ge(pvd[1], L1.U // 4 * (p - 1))
                            if due(L0.U // 4 * p):
                                act.wait_ge(pvd[0], L0.U // 4 * p)
                        else:
                            if due(L0.U // 4 * lim(p + 2)):
                                act.wait_ge(pvd[0], L0.U // 4 * lim(p + 2))
                    nc.scalar.activation(P[:, k % PR, :], exq[(k + 2 * i) % 3][:, :], ACT.Exp,
                                         scale=L.scale).then_inc(ex[i], 1)
                elif name == "pick":
                    if due(p + 1):
                        act.wait_ge(xsp, p + 1)
                    if due(2 * p):
                        act.wait_ge(hp, 2 * p)
                    if due(p):
                        act.wait_ge(x2p, p)
                    nc.scalar.copy(xsT[:, :, :].rearrange("p d k -> p (d k)"), pf[:, 0:256]).then_inc(xsc, 1)
                    nc.scalar.copy(ohT[:, :], pf[:, 256:384]).then_inc(xsc, 1)
                elif name == "gelu":
                    if due(2 * (p + 1)):
                        act.wait_ge(hz, 2 * (p + 1))
                    nc.scalar.activation(gz[:, :], z[:, :], ACT.Square).then_inc(g_sq, 1)
                    if due(2 * (p + 1)):
                        act.wait_ge(g_in, 2 * (p + 1))
                    nc.scalar.activation(gz[:, :], gz[:, :], ACT.Tanh, scale=GELU_C).then_inc(g_th, 1)
                elif name == "turn3":
                    if due(p + 1):
                        act.wait_ge(xtp, p + 1)
                    if due(OC * p):
                        act.wait_ge(gup, OC * p)
                    act.wait_ge(lku, LKN)
                    nc.scalar.copy(xT[:, :, :].rearrange("p d n -> p (d n)"), pf[:, :]).then_inc(xtc, 1)
                elif name == "up3":
                    if due(OC * p + k + 1):
                        act.wait_ge(gup, OC * p + k + 1)
                    if due(OC * p + max(k - 1, 0)):
                        act.wait_ge(s_ga, OC * p + max(k - 1, 0))
                    nc.scalar.activation(th[0:OM[k], k % 2, :], pf[0:OM[k], 0:T], ACT.Tanh, scale=0.5).then_inc(s_th, 1)

            program(act, step)

        @block.vector
        def _(dve):
            def norm(i, x, xn, p):
                n0 = 8 * p
                if due(n0):
                    dve.wait_ge(ln[i], n0)
                for b in range(NB):
                    nc.vector.bn_stats(stat[i][:, b, :], x[:, b, :]).then_inc(ln[i], 1)
                if due(n0 + 2):
                    dve.wait_ge(ln[i], n0 + 2)
                settle(dve, passed_dve)
                for b in range(NB):
                    nc.vector.bn_aggr(mv[i][:, b, :], stat[i][:, b, :]).then_inc(ln[i], 1)
                if due(n0 + 4):
                    dve.wait_ge(ln[i], n0 + 4)
                nc.vector.tensor_scalar(rstd[i][:, :], mv[i][:, :, 1], EPS, None, ALU.add).then_inc(ln[i], 1)
                if due(n0 + 5):
                    dve.wait_ge(ln[i], n0 + 5)
                if due(n0 + 6):
                    dve.wait_ge(ln[i], n0 + 6)
                for b in range(NB):
                    nc.vector.tensor_scalar(xn[:, b, :], x[:, b, :], mv[i][:, b, 0:1], rstd[i][:, b:b + 1],
                                            ALU.subtract, ALU.mult).then_inc(ln[i], 1)

            def lookup(c):
                w, c0, n = lookup_chunk(c)
                idx = w[:, c0:c0 + n].bitcast(U32)
                at = [LKC * c]

                def do(ins):
                    ins.then_inc(lku, 1)
                    at[0] += 1
                    dve.wait_ge(lku, at[0])

                m0, m1, m2, m3, t1, t2, t3 = (x[:, 0:n] for x in lk)
                do(nc.vector.tensor_scalar(m0.bitcast(I32), idx.bitcast(I32), 31, 31, ALU.logical_shift_left, ALU.arith_shift_right))
                for m, bit in ((m1, 2), (m2, 4), (m3, 8)):
                    do(nc.vector.tensor_scalar(m, idx, bit, None, ALU.bitwise_and))

                def leaf(dst, j):
                    do(nc.vector.tensor_scalar(dst, m0, lutx[:, j:j + 1], lut[:, 2 * j:2 * j + 1],
                                               ALU.bitwise_and, ALU.bitwise_xor))

                def four(dst, tmp, j):
                    leaf(dst, 2 * j)
                    leaf(tmp, 2 * j + 1)
                    do(nc.vector.copy_predicated(dst, m1, tmp))

                four(idx, t1, 0)
                four(t2, t1, 1)
                do(nc.vector.copy_predicated(idx, m2, t2))
                four(t2, t1, 2)
                four(t3, t1, 3)
                do(nc.vector.copy_predicated(t2, m2, t3))
                do(nc.vector.copy_predicated(idx, m3, t2))
                assert at[0] == LKC * (c + 1)

            nc.vector.memset(f32(KM[0][:, :, :]), 0.0).then_inc(set_z, 1)
            nc.vector.memset(ones[:, :], 1.0).then_inc(set_z, 1)
            nc.vector.memset(f32(KM[1][:, :, :]), 0.0).then_inc(set_z, 1)
            dve.wait_ge(s_tg, 1)
            nc.vector.tensor_tensor(tgx[:, 0:1], tg[:, 2:3], gts[:, 4:5], ALU.mult).then_inc(s_tg, 1)
            nc.vector.tensor_scalar(tgx[:, 1:2], tg[:, 3:4], 0.5, None, ALU.mult).then_inc(s_tg, 1)
            dve.wait_ge(ld_b, 16 * 5)
            lv = lut[:, :].rearrange("p (j two) -> p j two", two=2)
            nc.vector.tensor_tensor(lutx[:, :], lv[:, :, 0], lv[:, :, 1], ALU.bitwise_xor).then_inc(s_tg, 1)
            dve.wait_ge(s_tg, 4)
            dve.wait_ge(ld_i, 16 * 3)

            def step(name, p, k):
                if name == "norm0":
                    if due(64 * (p + 1)):
                        dve.wait_ge(ld_in, 64 * (p + 1))
                    if due(p):
                        dve.wait_ge(s_qp, p)
                    norm(0, xin, xn0, p)
                elif name == "norm1":
                    if due(p + 1):
                        dve.wait_ge(x2c, p + 1)
                    if due(4 * p):
                        dve.wait_ge(pl1, 4 * p)
                    norm(2, x2, xn1, p)
                elif name == "norm3":
                    if due(p + 1):
                        dve.wait_ge(xo[1], p + 1)
                    if due(16 * p):
                        dve.wait_ge(stored, 16 * p)
                    norm(3, x3, xnf1, p)
                elif name == "lookup":
                    lookup(k)
                elif name == "project0":
                    if due(16 * NASM[0] * p):
                        dve.wait_ge(asm[0], 16 * NASM[0] * p)
                    m = mrA[:, :, :].rearrange("p b t -> p (b t)")
                    nc.vector.tensor_scalar(mt[:, :], m[0:2, :], 1.0, None, ALU.mult).then_inc(pm, 1)
                    nc.vector.tensor_scalar(ngh[:, :], m[0:1, :], -1.0, NEG_HI, ALU.add, ALU.mult).then_inc(pm, 1)
                    nc.vector.tensor_scalar(ngl[:, :], m[0:1, :], -1.0, NEG_LO, ALU.add, ALU.mult).then_inc(pm, 1)
                    if due(p + 1):
                        dve.wait_ge(s_vp, p + 1)
                    if due(p):
                        dve.wait_ge(plv, p)
                    nc.vector.tensor_tensor(vf[:, :].rearrange("p (j n) -> p j n", j=4),
                                            pa[:, :].rearrange("p (j n) -> p j n", j=4),
                                            bv[:, :].unsqueeze(1).to_broadcast([128, 4, 128]), ALU.add).then_inc(s_vf, 1)
                elif name in ("max0", "max1"):
                    i, L = layer(name)
                    if due(L.U * p + k + 1):
                        dve.wait_ge(mp[i], L.U * p + k + 1)
                    if k == 0 and i == 0:
                        if due(p - 1):
                            dve.wait_ge(cp[1], p - 1)
                        if due(p):
                            dve.wait_ge(cp[0], p)
                    if k == 0 and i == 1:
                        if due(lim(p + 2)):
                            dve.wait_ge(cp[0], lim(p + 2))
                    h, b = k // 2, k % 2
                    nc.vector.tensor_reduce(mx[:, b, :, h], mxp[k % 2][:, :].rearrange("p (s t) -> p s t", s=2),
                                            AX.X, ALU.max).then_inc(md[i], 1)
                elif name in ("shift0", "shift1"):
                    i, L = layer(name)
                    if due(p + 1):
                        dve.wait_ge(ch[i], p + 1)
                    nc.vector.scalar_tensor_tensor(out=clo[0:L.H, :], in0=pa[0:L.H, :], scalar=-1.0,
                                                   in1=f32(chi[0:L.H, :]), op0=ALU.mult,
                                                   op1=ALU.subtract).then_inc(cl[i], 1)
                elif name in ("out0", "out1"):
                    i, L = layer(name)
                    if due(L.U // 4 * p + 2 * k + 2):
                        dve.wait_ge(pvd[i], L.U // 4 * p + 2 * k + 2)
                    if k >= 2:
                        if due(128 * (2 * p + 1)):
                            dve.wait_ge(oc[i][k % 2], 128 * (2 * p + 1))
                    elif i == 0:
                        if due(128 * (p - 1)):
                            dve.wait_ge(oc[1][k % 2], 128 * (p - 1))
                        if due(128 * 2 * p):
                            dve.wait_ge(oc[0][k % 2], 128 * 2 * p)
                    else:
                        if due(128 * 2 * lim(p + 2)):
                            dve.wait_ge(oc[0][k % 2], 128 * 2 * lim(p + 2))
                    nc.vector.tensor_copy(OG[:, k % 2, :], pv[:, :]).then_inc(og[i], 1)
                elif name in ("resid0", "resid1"):
                    i, L = layer(name)
                    for slot in range(2):
                        if due(128 * L.NT // 2 * (p + 1)):
                            dve.wait_ge(oc[i][slot], 128 * L.NT // 2 * (p + 1))
                    nc.vector.reciprocal(Dc[:, :], Dc[:, :]).then_inc(rc[i], 1)
                    if due(p + 1):
                        dve.wait_ge(rc[i], p + 1)
                    nc.vector.tensor_tensor(Oc[:, :], Oc[:, :], Dc[:, :], ALU.mult).then_inc(dv[i], 1)
                    flat = lambda t: t[:, :, :].rearrange("p b t -> p (b t)")
                    if i == 0:
                        if due(p + 1):
                            dve.wait_ge(om[0], p + 1)
                        if due(p + 1):
                            dve.wait_ge(xcp, p + 1)
                        if due(p):
                            dve.wait_ge(x2c, p)
                        dve.wait_ge(s_tg, 4)
                        nc.vector.scalar_tensor_tensor(out=flat(x1), in0=Oc[:, :], scalar=tg[:, 0:1], in1=flat(xr0),
                                                       op0=ALU.mult, op1=ALU.add).then_inc(xo[0], 1)
                    else:
                        if due(p + 1):
                            dve.wait_ge(dv[1], p + 1)
                        if due(p):
                            dve.wait_ge(x4c, p)
                        nc.vector.scalar_tensor_tensor(out=flat(x3), in0=Oc[:, :], scalar=tgx[:, 0:1], in1=flat(x2),
                                                       op0=ALU.mult, op1=ALU.add).then_inc(xo[1], 1)
                elif name == "route":
                    if due(p + 1):
                        dve.wait_ge(xo[0], p + 1)
                    if due(p):
                        dve.wait_ge(xsp, p)
                    norm(1, x1, xnf0, p)
                    if due(8 * (p + 1)):
                        dve.wait_ge(ln[1], 8 * (p + 1))
                    if due(p):
                        dve.wait_ge(rtp, p)
                    if due(12 * p):
                        dve.wait_ge(rt, 12 * p)
                    for b in range(NB):
                        if due(12 * p + b):
                            dve.wait_ge(rt, 12 * p + b)
                        settle(dve, passed_dve)
                        nc.vector.tensor_tensor_reduce(prod[:, :], xnf0[:, b, :], wr[:, :], 1.0, 0.0, ALU.mult,
                                                       ALU.add, rs[:, b, 0:1]).then_inc(rt, 1)
                    if due(12 * p + 2):
                        dve.wait_ge(rt, 12 * p + 2)
                    for b in range(NB):
                        nc.vector.tensor_scalar(rs[:, b, 1:2], rs[:, b, 0:1], br[:, 0:1], None, ALU.add).then_inc(rt, 1)
                    if due(12 * p + 4):
                        dve.wait_ge(rt, 12 * p + 4)
                    for b in range(NB):
                        nc.vector.tensor_scalar(sbc[:, b, :], tril[:, :], 0.0, rs[:, b, 1:2], ALU.mult,
                                                ALU.add).then_inc(rt, 1)
                elif name == "rank":
                    if due(p + 1):
                        dve.wait_ge(rtp, p + 1)
                    if due(p):
                        dve.wait_ge(xsp, p)
                    for b in range(NB):
                        row = pf[:, 128 * b:128 * b + 128]
                        nc.vector.tensor_scalar(prod[:, 0:128], row, rs[:, b, 1:2], None, ALU.is_gt).then_inc(rt, 1)
                        nc.vector.scalar_tensor_tensor(out=prod[:, 128:256], in0=row, scalar=rs[:, b, 1:2],
                                                       in1=tril[:, :], op0=ALU.is_equal, op1=ALU.mult).then_inc(rr, 1)
                        if due(2 * p + b + 1):
                            dve.wait_ge(rr, 2 * p + b + 1)
                        if due(12 * p + 7 + 3 * b):
                            dve.wait_ge(rt, 12 * p + 7 + 3 * b)
                        settle(dve, passed_dve)
                        nc.vector.tensor_tensor_reduce(prod[:, 0:128], prod[:, 0:128], prod[:, 128:256], 1.0, 0.0,
                                                       ALU.add, ALU.add, rs[:, b, 2:3]).then_inc(rt, 1)
                        if due(12 * p + 8 + 3 * b):
                            dve.wait_ge(rt, 12 * p + 8 + 3 * b)
                        nc.vector.tensor_scalar(oh[:, b, :], iota[:, :], rs[:, b, 2:3], None, ALU.is_equal).then_inc(rt, 1)
                elif name == "up2":
                    if due(2 * p + k + 1):
                        dve.wait_ge(hp, 2 * p + k + 1)
                    if due(p):
                        dve.wait_ge(yp, p)
                    nc.vector.tensor_tensor(z[:, 512 * k:512 * k + 512].rearrange("p (f n) -> p f n", f=4),
                                            pf[:, :].rearrange("p (f n) -> p f n", f=4),
                                            b1[:, 4 * k:4 * k + 4].unsqueeze(2).to_broadcast([128, 4, 128]),
                                            ALU.add).then_inc(hz, 1)
                elif name == "down2":
                    if due(p + 1):
                        dve.wait_ge(g_th, p + 1)
                    nc.vector.scalar_tensor_tensor(out=z[:, :], in0=gz[:, :], scalar=1.0, in1=z[:, :],
                                                   op0=ALU.add, op1=ALU.mult).then_inc(g_h, 1)
                    if due(p + 1):
                        dve.wait_ge(yp, p + 1)
                    if due(p):
                        dve.wait_ge(x2p, p)
                    nc.vector.scalar_tensor_tensor(out=y0[:, :], in0=pf[:, 0:T], scalar=0.5, in1=b2[:, :],
                                                   op0=ALU.mult, op1=ALU.add).then_inc(yc, 1)
                elif name == "add2":
                    if due(p + 1):
                        dve.wait_ge(x2p, p + 1)
                    if due(p):
                        dve.wait_ge(xo[1], p)
                    nc.vector.scalar_tensor_tensor(out=x2[:, :, :], in0=pf[:, :].rearrange("p (b t) -> p b t", b=NB),
                                                   scalar=tg[:, 1:2], in1=x1[:, :, :],
                                                   op0=ALU.mult, op1=ALU.add).then_inc(x2c, 1)
                elif name == "up3":
                    m = OM[k]
                    if due(OC * p + k + 1):
                        dve.wait_ge(s_th, OC * p + k + 1)
                    if due(OC * p + k):
                        dve.wait_ge(s_h1, OC * p + k)
                    nc.vector.scalar_tensor_tensor(out=ga1[0:m, :], in0=th[0:m, k % 2, :], scalar=1.0,
                                                   in1=pf[0:m, 0:T], op0=ALU.add, op1=ALU.mult).then_inc(s_ga, 1)
                    if due(OC * p + k + 1):
                        dve.wait_ge(s_ga, OC * p + k + 1)
                    if due(p):
                        dve.wait_ge(dnp, p)
                    nc.vector.tensor_tensor(h1[0:m, k, :], ga1[0:m, :], pf[0:m, T:2 * T], ALU.mult).then_inc(s_h1, 1)
                elif name == "down3":
                    if due(p + 1):
                        dve.wait_ge(dnp, p + 1)
                    nc.vector.scalar_tensor_tensor(out=xnf1[:, :, :], in0=pf[:, :].rearrange("p (b t) -> p b t", b=NB),
                                                   scalar=tgx[:, 1:2], in1=x3[:, :, :],
                                                   op0=ALU.mult, op1=ALU.add).then_inc(x4c, 1)

            program(dve, step)

        @block.gpsimd
        def _(pool):
            for i, L in enumerate((L0, L1)):
                nc.gpsimd.memset(V[i][:, :, :, L.DH:32], 0.0).then_inc(set_v, 1)
            nc.gpsimd.memset(mhalf[:, :], -0.5).then_inc(set_v, 1)
            pool.wait_ge(set_v, 3)
            for i, L in enumerate((L0, L1)):
                nc.gpsimd.memset(V[i][:, :, :, L.DH:2 * L.DH], 1.0).then_inc(set_z, 1)

            def split(src, hi, lo, sm, n):
                settle(pool, passed_pool)
                nc.gpsimd.tensor_scalar(hi, src, 1.0, None, ALU.mult).then_inc(sm, 1)
                if due(n):
                    pool.wait_ge(sm, n)
                nc.gpsimd.tensor_tensor(lo, src, f32(hi), ALU.subtract).then_inc(sm, 1)

            def step(name, p, k):
                flat = lambda t: t[:, :, :].rearrange("p b t -> p (b t)")
                if name in ("norm0", "route", "norm1", "norm3"):
                    i = ("norm0", "route", "norm1", "norm3").index(name)
                    if due(8 * p + 5):
                        pool.wait_ge(ln[i], 8 * p + 5)
                    nc.gpsimd.tensor_tensor(rstd[i][:, :], rstd[i][:, :], mhalf[:, :], ALU.pow).then_inc(ln[i], 1)
                elif name == "project0":
                    if due(64 * (p + 1)):
                        pool.wait_ge(ld_in, 64 * (p + 1))
                    if due(16 * NASM[0] * p):
                        pool.wait_ge(asm[0], 16 * NASM[0] * p)
                    if due(16 * NASM[1] * (p - 1)):
                        pool.wait_ge(asm[1], 16 * NASM[1] * (p - 1))
                    m = flat(mrA)
                    for j, (t, done, hi, lo) in enumerate(((qf, s_qf, qh, ql), (kf, s_kf, kh, kl))):
                        if due(p + 1):
                            pool.wait_ge(done, p + 1)
                        nc.gpsimd.tensor_tensor(t[:, :], t[:, :], m, ALU.mult).then_inc(pl0, 1)
                        if due(6 * p + 3 * j + 1):
                            pool.wait_ge(pl0, 6 * p + 3 * j + 1)
                        split(t[:, :], hi[:, :], lo[:, :], pl0, 6 * p + 3 * j + 2)
                elif name == "values0":
                    if due(p + 1):
                        pool.wait_ge(s_vf, p + 1)
                    if due(L0.U // 4 * p):
                        pool.wait_ge(pvd[0], L0.U // 4 * p)
                    nc.gpsimd.tensor_tensor(V[0][:, :, :, 0:L0.DH], vf[:, :].rearrange("p (j h d) -> p j h d", j=4, h=L0.H),
                                            mc[:, :].unsqueeze(2).unsqueeze(3).to_broadcast([128, 4, L0.H, L0.DH]),
                                            ALU.mult).then_inc(plv, 1)
                elif name == "split1":
                    if due(8 * (p + 1)):
                        pool.wait_ge(ln[2], 8 * (p + 1))
                    if due(16 * (p + 1)):
                        pool.wait_ge(ld_c1, 16 * (p + 1))
                    if due(16 * NASM[0] * lim(p + 2)):
                        pool.wait_ge(asm[0], 16 * NASM[0] * lim(p + 2))
                    split(flat(xn1), qh[:, :], ql[:, :], pl1, 4 * p + 1)
                    split(flat(ctx1), kh[:, :], kl[:, :], pl1, 4 * p + 3)
                elif name == "keep0":
                    if due(8 * (p + 1)):
                        pool.wait_ge(ln[0], 8 * (p + 1))
                    if due(p):
                        pool.wait_ge(xo[0], p)
                    settle(pool, passed_pool)
                    nc.gpsimd.tensor_scalar(flat(xr0), flat(xin), 1.0, None, ALU.mult).then_inc(xcp, 1)
                elif name == "resid0":
                    if due(p + 1):
                        pool.wait_ge(dv[0], p + 1)
                    if due(16 * (p + 1)):
                        pool.wait_ge(ld_mb, 16 * (p + 1))
                    nc.gpsimd.tensor_tensor(Oc[:, :], Oc[:, :], flat(mrB), ALU.mult).then_inc(om[0], 1)
                elif name == "gelu":
                    if due(p + 1):
                        pool.wait_ge(g_sq, p + 1)
                    settle(pool, passed_pool)
                    nc.gpsimd.tensor_scalar(gz[:, :], gz[:, :], 0.044715, 1.0, ALU.mult, ALU.add).then_inc(g_in, 1)
                    if due(2 * p + 1):
                        pool.wait_ge(g_in, 2 * p + 1)
                    nc.gpsimd.tensor_tensor(gz[:, :], gz[:, :], z[:, :], ALU.mult).then_inc(g_in, 1)

            program(pool, step)


def kernel(**inputs):
    import numpy as _np
    import concourse.bacc as _bacc
    from concourse import mybir as _mybir
    from concourse.bass_utils import run_bass_kernel_spmd as _run

    v = {k: _np.asarray(x) for k, x in inputs.items()}
    chunks = lambda w, n: _np.pad(w, ((0, n * 128 - w.shape[0]), (0, 0))).reshape(n, 128, -1).transpose(1, 0, 2)
    laid = {
        "x": v["x"], "ctx_2048": v["ctx_2048"],
        "wqT": v["L0_xattn_Wq"].T, "wkT": v["L0_xattn_Wk"].T, "wvT": v["L0_xattn_Wv"].T,
        "bqk": _np.stack([v["L0_xattn_bq"], v["L0_xattn_bk"]], 1), "L0_xattn_bv": v["L0_xattn_bv"],
        "gts": _np.stack([v["g_xattn"][0], v["g_ffn"][0], v["g_xattn"][1], v["g_ffn"][1],
                          v["L1_xattn_gamma"]]).reshape(1, 5),
        "mrow": v["mask_Bx1x2048_fk1"].reshape(NP, N),
        "mcol": v["mask_Bx1x2048_fk1"].reshape(NP, NB * 2, 128).transpose(0, 2, 1),
        "L0_ffn_w_r": v["L0_ffn_w_r"], "br": v["L0_ffn_b_r"].reshape(1, 1),
        "L0_ffn_w1": v["L0_ffn_w1"], "b1c": v["L0_ffn_b1"].reshape(FC, 128).T,
        "L0_ffn_w2": v["L0_ffn_w2"], "L0_ffn_b2": v["L0_ffn_b2"],
        "L1_ffn_lut": v["L1_ffn_lut"],
        "gate_i": chunks(v["L1_ffn_gate_idx"].T, 2), "up_i": chunks(v["L1_ffn_up_idx"].T, 2),
        "down_i": chunks(v["L1_ffn_down_idx"].T, OC),
        "ident": _np.eye(128, dtype=_np.float32), "tril": _np.tril(_np.ones((128, 128), _np.float32), -1),
        "iota": _np.arange(KEEP, dtype=_np.float32).reshape(1, KEEP),
    }
    nc = _bacc.Bacc("TRN2", target_bir_lowering=False, num_devices=1)
    arrays, aps = {}, {}
    for name, x in laid.items():
        x = _np.ascontiguousarray(x)
        arrays[f"in_{name}"] = x
        aps[name] = nc.dram_tensor(f"in_{name}", x.shape, _mybir.dt.from_np(x.dtype), kind="ExternalInput").ap()
    out = nc.dram_tensor("out", (B, C, T), _mybir.dt.from_np(_np.dtype("float32")), kind="ExternalOutput").ap()
    flamingo_kernel(nc, aps, out)
    r = _run(nc, [arrays], core_ids=[0])
    return r.results[0]["out"]
```

```python
from contextlib import ExitStack

import numpy as np

import concourse.bass as bass
from concourse import mybir

F32 = mybir.dt.float32
F32R = mybir.dt.float32r
I32 = mybir.dt.int32
U32 = mybir.dt.uint32
ALU = mybir.AluOpType
ACT = mybir.ActivationFunctionType
AX = mybir.AxisListType

B, C, T = 16, 128, 256
NB = 2
NP = B // NB
N = NB * T
DF, FC = 1024, 8
INTER, OC = 688, 6
OM = [min(128, INTER - 128 * o) for o in range(OC)]
KEEP = 64
LUT = 16
EPS = 1e-5
NEG = 1e6
GELU_C = float(np.sqrt(2.0 / np.pi))


class Layer:

    def __init__(self, heads, masked):
        self.H = heads
        self.DH = 128 // heads
        self.HPG = 32 // self.DH
        self.NG = 4
        self.SHIFT = 98 if masked else 96
        self.KE = self.SHIFT + 2 * self.HPG
        self.U = heads * NB
        self.NT = heads // 4
        self.scale = 1.0 / float(np.sqrt(self.DH))


L0 = Layer(16, True)
L1 = Layer(8, False)
NEG0 = NEG / L0.scale
NEG_HI = float(np.round(NEG0 / 2048) * 2048)
NEG_LO = NEG0 - NEG_HI


PAIR = {"m0": 1, "e0": 0, "f0": 0, "m1": -1, "e1": -1, "f1": -2}

STEPS = (
    ("exp0", "e0", L0.U, -0.1, 1.006),
    ("max1", "m1", L1.U, 13.12, 0.981),
    ("pv0", "e0", L0.U // 4 - 1, 6.2, 4),
    ("out0", "e0", L0.NT - 1, 10.34, 8.961),
    ("stats1", "m1", 1, 0.4, 0), ("stats3", "f1", 1, 0.5, 0), ("scale1", "m1", 1, 1.4, 0), ("load", "m0", 1, 1.5, 0),
    ("scale3", "f1", 1, 2.4, 0), ("split1", "m1", 1, 2.5, 0), ("turn3", "f1", 1, 3.4, 0), ("store1", "m1", 1, 4.4, 0),
    ("turned3", "f1", 1, 2.53, 0), ("values1", "m1", 1, 2.36, 0), ("values1b", "m1", 1, 6.4, 0),
    ("assemble1", "m1", 1, 9.94, 0), ("keys1", "m1", L1.HPG, 3.8, 0.1),
    ("stats0", "m0", 1, 7.4, 0), ("scale0", "m0", 1, 8.63, 0), ("masks0", "m0", 1, 8.5, 0),
    ("query0", "m0", 1, 11.04, 0), ("query0b", "m0", 1, 12.4, 0), ("key0", "m0", 1, 13.4, 0), ("key0b", "m0", 1, 14.97, 0),
    ("value0", "m0", 1, 16.4, 0), ("split0", "m0", 1, 17.4, 0), ("value0b", "m0", 1, 17.53, 0),
    ("store0", "m0", 1, 27.92, 0), ("turnmax1", "m1", 1, 29.5, 0), ("shift1", "m1", 1, 29.28, 0),
    ("up3", "f1", OC, 4.75, 4.032), ("tanh3", "f1", OC, 7.8, 3.171), ("hidden3", "f1", OC, 8.7, 3.169),
    ("assemble0", "m0", 1, 30.67, 0), ("keys0", "m0", L0.HPG, 17.48, 1.032),
    ("pv0last", "e0", 1, 32.2, 0), ("out0last", "e0", 1, 31.9, 0), ("down3", "f1", 1, 32.4, 0),
    ("gather0", "e0", 1, 34.2, 0), ("values0", "m0", 1, 35.2, 0), ("invert0", "e0", 1, 38, 0), ("add3", "f1", 1, 40.25, 0),
    ("exp1", "e1", 4, 37.35, 0.108), ("exp1more", "e1", L1.U - 4, 41.35, 1.5),
    ("max0", "m0", L0.U, 39.85, 1.01),
    ("pv1", "e1", L1.U // 4 - 1, 43.2, 6), ("out1", "e1", 1, 50.2, 0),
    ("pv1last", "e1", 1, 61.3, 0), ("out1last", "e1", 1, 62.3, 0), ("gather1", "e1", 1, 63.74, 0),
    ("invert1", "e1", 1, 69.63, 0), ("resid1", "e1", 1, 72.83, 0),
    ("resid0", "e0", 1, 45.3, 0), ("keep0", "m0", 1, 51.38, 0), ("skip0", "e0", 1, 48.3, 0),
    ("stats2", "f0", 1, 49.3, 0), ("scale2", "f0", 1, 50.04, 0), ("rank", "f0", 1, 52.3, 0), ("onehot", "f0", 1, 53.3, 0),
    ("pick", "f0", 1, 55.3, 0), ("picked", "f0", 1, 56.3, 0), ("up2", "f0", 2, 58.89, 2), ("bias2", "f0", 2, 58.19, 2.028),
    ("square2", "f0", 1, 61.88, 0), ("inner2", "f0", 1, 66.52, 0), ("tanh2", "f0", 1, 66.4, 0), ("gelu2", "f0", 1, 68.3, 0),
    ("turnmax0", "m0", 1, 72.78, 0), ("shift0", "m0", 1, 72.1, 0),
    ("down2", "f0", 1, 73.68, 0), ("half2", "f0", 1, 74, 0), ("spread", "f0", 1, 74.36, 0), ("add2", "f0", 1, 76, 0),
)

LAG = {
    ("act", "down3"): 2.16,
    ("act", "turnmax1"): 0.93,
    ("dve", "scale3"): 0.77,
    ("dve", "store1"): 4.96,
    ("pe", "shift0"): -0.17,
    ("pool", "value0b"): -0.33,
    ("sp", "down2"): 0.46,
    ("sp", "down3"): 0.01,
    ("sp", "keys0"): 14.57,
    ("sp", "keys1"): 6.19,
}

LOOKUPS = (
    (-1, -0.07), (-1, 11.69), (-1, 11.79), (-1, 77.39), (0, 19.5), (0, 34.25), (0, 42.46), (0, 44.21), (1, 33.99), (1, 49.71), (1, 57.5), (1, 63.55),
)


def lim(count):
    return min(count, NP) if isinstance(count, int) else count


def due(count):
    return not isinstance(count, int) or count > 0


def settle(eng, passed, count=None):
    if not isinstance(count, int):
        eng.sem_inc(passed, 1)


def flamingo_kernel(nc, a, out):
    with ExitStack() as ctx:
        def sb(name, shape, dt=F32):
            return ctx.enter_context(nc.sbuf_tensor(name, shape, dt))

        def ps(name):
            return ctx.enter_context(nc.psum_tensor(name, [128, 512], F32))

        def sem(name):
            return ctx.enter_context(nc.semaphore(name))

        ident = sb("ident", [128, 128])
        tril = sb("tril", [128, 128])
        iota = sb("iota", [128, KEEP])
        wq, wk, wv = sb("wq", [128, 128]), sb("wk", [128, 128]), sb("wv", [128, 128])
        bqk = sb("bqk", [128, 2])
        bv = sb("bv", [128, 128])
        wr = sb("wr", [128, T])
        br = sb("br", [128, 1])
        w1 = sb("w1", [128, 2, DF])
        b1 = sb("b1", [128, FC])
        w2 = sb("w2", [128, FC, T])
        b2 = sb("b2", [128, T])
        wg = sb("wg", [128, 2, INTER])
        wu = sb("wu", [128, 2, INTER])
        wd = sb("wd", [128, OC, T])
        lut = sb("lut", [128, LUT], U32)
        lutx = sb("lutx", [128, LUT // 2], U32)
        gts = sb("gts", [128, 5])
        tg = sb("tg", [128, 4])
        tgx = sb("tgx", [128, 2])

        mhalf = sb("mhalf", [128, NB])
        xin, xr0, x1, x2, x3 = (sb(n, [128, NB, T]) for n in ("xin", "xr0", "x1", "x2", "x3"))
        ctx0, ctx1 = sb("ctx0", [128, NB, T]), sb("ctx1", [128, NB, T])
        xn0, xnf0, xn1, xnf1 = (sb(n, [128, NB, T]) for n in ("xn0", "xnf0", "xn1", "xnf1"))
        mrA, mrB = sb("mrA", [128, NB, T]), sb("mrB", [128, NB, T])
        mc = sb("mc", [128, NB * 2])
        stat = [sb(f"stat{i}", [128, NB, 6]) for i in range(4)]
        mv = [sb(f"mv{i}", [128, NB, 2]) for i in range(4)]
        rstd = [sb(f"rstd{i}", [128, NB]) for i in range(4)]

        qf = sb("qf", [128, N])
        kf = sb("kf", [128, N])
        vf = sb("vf", [128, N])
        qhl, khl = sb("qhl", [128, 2, N], F32R), sb("khl", [128, 2, N], F32R)
        mrows, srows = sb("mrows", [128, N]), sb("srows", [128, N])
        ng = mrows[0:2, :].bitcast(F32R)
        mt = mrows[32:34, :].bitcast(F32R)
        negs = sb("negs", [2, 1])
        chi, clo = srows[0:L0.H, :].bitcast(F32R), srows[32:32 + L0.H, :].bitcast(F32R)
        ones = srows[64:66, :]
        QT = [sb(f"QT{i}", [128, L.NG, N], F32R) for i, L in enumerate((L0, L1))]
        KM = [sb(f"KM{i}", [128, L.H, N], F32R) for i, L in enumerate((L0, L1))]
        V = [sb(f"V{i}", [128, 2 * NB, L.H, 32]) for i, L in enumerate((L0, L1))]
        mx = sb("mx", [128, NB, 2, L0.H])
        PR = 8
        P = sb("P", [128, PR, 512])
        OG = sb("OG", [128, 2, 512])
        Oc, Dc = sb("Oc", [128, N]), sb("Dc", [128, N])
        Dn = sb("Dn", [128, 64])

        def scratch(name, shape):
            return nc.dram_tensor(name, shape, F32, kind="Internal").ap()

        q_parts = [scratch(f"q_parts{i}", (2, 128, N)) for i in range(2)]
        k_parts = [scratch(f"k_parts{i}", (2, 128, N)) for i in range(2)]
        shifts = [scratch(f"shifts{i}", (L.H, 2, N)) for i, L in enumerate((L0, L1))]
        outputs = [scratch(f"outputs{i}", (L.H, 32, N)) for i, L in enumerate((L0, L1))]
        recips = [scratch(f"recips{i}", (L.H, N)) for i, L in enumerate((L0, L1))]

        rs = sb("rs", [128, NB, 4])
        prod = sb("prod", [128, T])
        sbc = sb("sbc", [128, NB, 128])
        oh = sb("oh", [128, NB, KEEP])
        ohT = sb("ohT", [128, 128])
        xsT = sb("xsT", [128, 2, 128])
        z = sb("z", [128, DF])
        gz = sb("gz", [128, DF])
        y0 = sb("y0", [128, T])

        arena = sb("arena", [128, 2816])
        h1 = arena[:, 0:1536].rearrange("p (o n) -> p o n", o=OC)
        xT = arena[:, 1536:2048].rearrange("p (d n) -> p d n", d=2)
        th = arena[:, 2048:2560].rearrange("p (k n) -> p k n", k=2)
        ga1 = arena[:, 2560:2816]
        CH = 384
        lk = [arena[:, CH * j:CH * (j + 1)].bitcast(U32) for j in range(7)]

        mxp = [ps("mxp0"), ps("mxp1")]
        exq = [ps("exq0"), ps("exq1"), ps("exq2")]
        pv = ps("pv")
        pa = ps("pa")
        pf = ps("pf")

        ld_w, ld_b, ld_m, ld_i = sem("ld_w"), sem("ld_b"), sem("ld_m"), sem("ld_i")
        ld_in, ld_c1, ld_mb = sem("ld_in"), sem("ld_c1"), sem("ld_mb")
        set_z, set_o = sem("set_z"), sem("set_o")
        s_tg = sem("s_tg")
        lku = sem("lku")
        ln = [sem(f"ln{i}") for i in range(4)]
        xcp = sem("xcp")
        s_qp, s_qf, s_kp, s_kf, s_vp, s_vf = (sem(n) for n in ("s_qp", "s_qf", "s_kp", "s_kf", "s_vp", "s_vf"))
        pl0, pl1, pm, plv = sem("pl0"), sem("pl1"), sem("pm"), sem("plv")
        v1p, v1c = sem("v1p"), sem("v1c")
        qw, kw, qa, ma = ([sem(f"{n}{i}") for i in range(2)] for n in ("qw", "kw", "qa", "ma"))
        ka = [[sem(f"ka{i}{g}") for g in range(L.HPG)] for i, L in enumerate((L0, L1))]
        mp, md = [sem("mp0"), sem("mp1")], [sem("md0"), sem("md1")]
        cp, ch, cl, cw, cd = ([sem(f"{n}{i}") for i in range(2)] for n in ("cp", "ch", "cl", "cw", "cd"))
        sc, ex, pvd, og = ([sem(f"{n}{i}") for i in range(2)] for n in ("sc", "ex", "pvd", "og"))
        ow = [[sem(f"ow{i}{j}") for j in range(2)] for i in range(2)]
        dr, ocr, rw, dcr = ([sem(f"{n}{i}") for i in range(2)] for n in ("dr", "ocr", "rw", "dcr"))
        rc, dv, om, xo = ([sem(f"{n}{i}") for i in range(2)] for n in ("rc", "dv", "om", "xo"))
        rt, rtp, rr, set_v = sem("rt"), sem("rtp"), sem("rr"), sem("set_v")
        xsp, xsc, hp, hz = sem("xsp"), sem("xsc"), sem("hp"), sem("hz")
        g_sq, g_in, g_th, g_h = sem("g_sq"), sem("g_in"), sem("g_th"), sem("g_h")
        yp, yc, x2q, x2p, x2c = (sem(n) for n in ("yp", "yc", "x2q", "x2p", "x2c"))
        xtp, xtc, gup, s_th, s_ga, s_h1 = (sem(n) for n in ("xtp", "xtc", "gup", "s_th", "s_ga", "s_h1"))
        passed_sp, passed_dve, passed_pool = sem("passed_sp"), sem("passed_dve"), sem("passed_pool")
        dnp, x4c, stored = sem("dnp"), sem("x4c"), sem("stored")

        def f32(ap):
            return ap.bitcast(F32)

        block = ctx.enter_context(nc.Block())


        def unit(k):
            return 4 * (k // 8) + k % 4, k // 4 % 2

        def max_unit(L, k):
            g, G = k // (2 * L.NG), k // 2 % L.NG
            return L.HPG * G + g, k % 2, g

        LKC = 19
        LKN = LKC * 12

        def lookup_chunk(c):
            if c < 8:
                w = (wg, wu)[c // 4]
                return w[:, :, :].rearrange("p d n -> p (d n)"), (c % 4) * 344, 344
            return wd[:, :, :].rearrange("p o n -> p (o n)"), (c - 8) * 384, 384

        def steps(engine, i, **there):
            plan = [(at + LAG.get((engine, name), 0) + apart * k, name, i + PAIR[stage], k)
                    for name, stage, parts, at, apart in STEPS if there.get(stage, True) for k in range(parts)]
            plan += [(at, "lookup", 0, k) for k, (when, at) in enumerate(LOOKUPS) if isinstance(i, int) and when == i]
            for _, name, p, k in sorted(plan, key=lambda s: s[0]):
                name, k = whole(name, k)
                yield name, p, k

        def program(engine, eng, step):
            for i in (-1, 0, 1, 2):
                for name, p, k in steps(engine, i, e0=i >= 0, f0=i >= 0, m1=i >= 1, e1=i >= 1, f1=i >= 2):
                    step(name, p, k)
            with eng.Fori(3, NP - 1) as i:
                for name, p, k in steps(engine, i):
                    step(name, p, k)
            for i in (NP - 1, NP, NP + 1):
                for name, p, k in steps(engine, i, m0=False, e0=i < NP, f0=i < NP, m1=i <= NP, e1=i <= NP):
                    step(name, p, k)

        def layer(name):
            i = int(name[-1])
            return i, (L0, L1)[i]

        def whole(name, k):
            if name.endswith("last"):
                name = name[:-4]
                return name, {"pv0": L0.U // 4, "pv1": L1.U // 4, "out0": L0.NT, "out1": L1.NT}[name] - 1
            return (name[:-4], k + 4) if name.endswith("more") else (name, k)

        @block.sync
        def _(sp):
            def rows(ap):
                return ap.rearrange("(a d) -> a d", a=1)

            def inputs0(p):
                if due(p):
                    sp.wait_ge(xcp, p)
                settle(sp, passed_sp, p)
                if due(p):
                    sp.wait_ge(s_vp, p)
                settle(sp, passed_sp, p)
                if due(p):
                    sp.wait_ge(plv, p)
                settle(sp, passed_sp, p)
                if due(2 * p):
                    sp.wait_ge(pm, 2 * p)
                settle(sp, passed_sp, 2 * p)
                if due(6 * p):
                    sp.wait_ge(pl0, 6 * p)
                settle(sp, passed_sp, 6 * p)
                pair = bass.ds(p * NB, NB)
                sp.dma_start(xin[:, :, :], a["x"][pair].rearrange("b c t -> c b t")).then_inc(ld_in, 16)
                sp.dma_start(ctx0[:, :, :], a["ctx_2048"][pair].rearrange("b c t -> c b t")).then_inc(ld_in, 16)
                sp.dma_start(mrA[:, :, :].rearrange("p b t -> p (b t)"),
                             a["mrow"][bass.ds(p, 1), :].to_broadcast([128, N])).then_inc(ld_in, 16)
                sp.dma_start(mc[:, :], a["mcol"][bass.ds(p, 1)].rearrange("a p k -> (a p) k")).then_inc(ld_in, 16)

            def context1(p):
                if due(4 * p):
                    sp.wait_ge(pl1, 4 * p)
                settle(sp, passed_sp, 4 * p)
                if due(p):
                    sp.wait_ge(v1p, p)
                settle(sp, passed_sp, p)
                sp.dma_start(ctx1[:, :, :], a["ctx_2048"][bass.ds(p * NB, NB)].rearrange("b c t -> c b t")).then_inc(ld_c1, 16)

            def target_mask(p):
                if due(p):
                    sp.wait_ge(om[0], p)
                settle(sp, passed_sp, p)
                sp.dma_start(mrB[:, :, :].rearrange("p b t -> p (b t)"),
                             a["mrow"][bass.ds(p, 1), :].to_broadcast([128, N])).then_inc(ld_mb, 16)

            for dst, src in ((ident, a["ident"]), (wq, a["wqT"]), (wk, a["wkT"]), (wv, a["wvT"]), (bqk, a["bqk"])):
                sp.dma_start(dst[:, :], src).then_inc(ld_w, 16)
            sp.dma_start(bv[:, :], rows(a["L0_xattn_bv"]).to_broadcast([128, 128])).then_inc(ld_w, 16)
            sp.dma_start(gts[:, :], a["gts"].to_broadcast([128, 5])).then_inc(ld_w, 16)
            sp.dma_start(negs[:, :], a["negs"]).then_inc(ld_w, 16)
            sp.dma_start(tril[:, :], a["tril"]).then_inc(ld_b, 16)
            sp.dma_start(iota[:, :], a["iota"].to_broadcast([128, KEEP])).then_inc(ld_b, 16)
            sp.dma_start(wr[:, :], rows(a["L0_ffn_w_r"]).to_broadcast([128, T])).then_inc(ld_b, 16)
            sp.dma_start(br[:, :], a["br"].to_broadcast([128, 1])).then_inc(ld_b, 16)
            sp.dma_start(lut[:, :], rows(a["L1_ffn_lut"]).to_broadcast([128, LUT]).bitcast(U32)).then_inc(ld_b, 16)
            sp.dma_start(wg[:, :, :].bitcast(I32), a["gate_i"]).then_inc(ld_i, 16)
            sp.dma_start(wu[:, :, :].bitcast(I32), a["up_i"]).then_inc(ld_i, 16)
            sp.dma_start(wd[:, :, :].bitcast(I32), a["down_i"]).then_inc(ld_i, 16)
            sp.wait_ge(set_z, 5)
            for L, km in ((L0, KM[0]), (L1, KM[1])):
                for g in range(L.HPG):
                    r = L.SHIFT + 2 * g
                    sp.dma_start(f32(km[r:r + 2, g::L.HPG, :]),
                                 ones[:, :].unsqueeze(1).to_broadcast([2, L.NG, N])).then_inc(set_o, 16)
            sp.dma_start(w1[:, :, :], a["L0_ffn_w1"].rearrange("(k p) n -> p k n", p=128)).then_inc(ld_m, 16)
            sp.dma_start(b1[:, :], a["b1c"]).then_inc(ld_m, 16)
            sp.dma_start(w2[:, :, :], a["L0_ffn_w2"].rearrange("(k p) n -> p k n", p=128)).then_inc(ld_m, 16)
            sp.dma_start(b2[:, :], rows(a["L0_ffn_b2"]).to_broadcast([128, T])).then_inc(ld_m, 16)

            def step(name, p, k):
                if name in ("store0", "store1"):
                    i, L = layer(name)
                    for half, (src, dst, written, read) in enumerate(((qhl, q_parts, qw, qa), (khl, k_parts, kw, ka))):
                        done = (6, 4)[i] * p + ((3, 6), (2, 4))[i][half]
                        sp.wait_ge((pl0, pl1)[i], done)
                        settle(sp, passed_sp, done)
                        if half == 0:
                            if due(p):
                                sp.wait_ge(qa[i], 48 * p)
                            settle(sp, passed_sp, p)
                        else:
                            for g in range(L.HPG):
                                if due(p):
                                    sp.wait_ge(ka[i][g], 48 * p)
                                settle(sp, passed_sp, p)
                        sp.dma_start(dst[i].rearrange("j p n -> p j n"), f32(src[:, :, :])).then_inc(written[i], 16)
                elif name in ("assemble0", "assemble1"):
                    i, L = layer(name)
                    sp.wait_ge(qw[i], 16 * (p + 1))
                    settle(sp, passed_sp, p)
                    if due(L.U * p):
                        sp.wait_ge(sc[i], L.U * p)
                    settle(sp, passed_sp, p)
                    q = q_parts[i].rearrange("j (G p) n -> j p G n", G=L.NG)
                    for j, part in enumerate((0, 0, 1)):
                        sp.dma_start(f32(QT[i][32 * j:32 * j + 32, :, :]), q[part]).then_inc(qa[i], 16)
                    if i == 0:
                        sp.wait_ge(pm, 2 * (p + 1))
                        settle(sp, passed_sp, p)
                        sp.dma_start(f32(QT[0][96:98, :, :]),
                                     f32(mt[:, :]).unsqueeze(1).to_broadcast([2, L.NG, N])).then_inc(ma[0], 16)
                        sp.dma_start(f32(KM[0][96:98, :, :]),
                                     f32(ng[:, :]).unsqueeze(1).to_broadcast([2, L.H, N])).then_inc(ma[0], 16)
                elif name in ("keys0", "keys1"):
                    i, L = layer(name)
                    if k == 0:
                        sp.wait_ge(kw[i], 16 * (p + 1))
                        settle(sp, passed_sp, p)
                        if due(L.U * p):
                            sp.wait_ge(sc[i], L.U * p)
                        settle(sp, passed_sp, p)
                    keys = k_parts[i].rearrange("j (G g d) n -> j g d G n", G=L.NG, g=L.HPG)
                    for j, part in enumerate((0, 1, 0)):
                        r = 32 * j + L.DH * k
                        sp.dma_start(f32(KM[i][r:r + L.DH, k::L.HPG, :]), keys[part, k]).then_inc(ka[i][k], 16)
                elif name in ("shift0", "shift1"):
                    i, L = layer(name)
                    sp.wait_ge(cl[i], p + 1)
                    settle(sp, passed_sp, p)
                    if due(p):
                        sp.wait_ge(cd[i], 16 * p)
                    settle(sp, passed_sp, p)
                    for j, src in enumerate((chi, clo)):
                        sp.dma_start(shifts[i][:, j, :], f32(src[0:L.H, :])).then_inc(cw[i], 16)
                    sp.wait_ge(cw[i], 32 * (p + 1))
                    settle(sp, passed_sp, p)
                    sp.dma_start(f32(QT[i][L.SHIFT:L.KE, :, :]),
                                 shifts[i].rearrange("(G g) j n -> (g j) G n", G=L.NG)).then_inc(cd[i], 16)
                elif name in ("out0", "out1"):
                    i, L = layer(name)
                    sp.wait_ge(og[i], L.NT * p + k + 1)
                    settle(sp, passed_sp, p)
                    if k == 0:
                        if due(p):
                            sp.wait_ge(ocr[i], 16 * p)
                        settle(sp, passed_sp, p)
                        if due(p):
                            sp.wait_ge(dr[i], 16 * p)
                        settle(sp, passed_sp, p)
                    sp.dma_start(outputs[i][4 * k:4 * k + 4].rearrange("h c n -> (h c) n"),
                                 OG[:, k % 2, :]).then_inc(ow[i][k % 2], 16)
                elif name in ("gather0", "gather1"):
                    i, L = layer(name)
                    for slot in range(2):
                        sp.wait_ge(ow[i][slot], 8 * L.NT * (p + 1))
                        settle(sp, passed_sp, p)
                    if i == 0:
                        if due(p - 1):
                            sp.wait_ge(xo[1], p - 1)
                        settle(sp, passed_sp, p - 1)
                        if due(p):
                            sp.wait_ge(xo[0], p)
                        settle(sp, passed_sp, p)
                    else:
                        sp.wait_ge(xo[0], lim(p + 2))
                        settle(sp, passed_sp, p)
                    w = L.H * N // 128
                    sp.dma_start(Dn[:, 0:w], outputs[i][:, L.DH, :].rearrange("h (j n) -> h j n", n=w)).then_inc(dr[i], 16)
                    sp.dma_start(Oc[:, :], outputs[i][:, 0:L.DH, :]).then_inc(ocr[i], 16)
                elif name in ("invert0", "invert1"):
                    i, L = layer(name)
                    w = L.H * N // 128
                    sp.wait_ge(rc[i], p + 1)
                    settle(sp, passed_sp, p)
                    sp.dma_start(recips[i].rearrange("h (j n) -> h j n", n=w), Dn[:, 0:w]).then_inc(rw[i], 16)
                    sp.wait_ge(rw[i], 16 * (p + 1))
                    settle(sp, passed_sp, p)
                    sp.dma_start(Dc[:, :], recips[i].unsqueeze(1).to_broadcast([L.H, L.DH, N])).then_inc(dcr[i], 16)
                elif name == "load":
                    inputs0(p)
                elif name == "keep0":
                    target_mask(p)
                elif name == "skip0":
                    context1(p)
                elif name == "add3":
                    sp.wait_ge(x4c, p + 1)
                    settle(sp, passed_sp, p + 1)
                    sp.dma_start(out[bass.ds(p * NB, NB)].rearrange("b c t -> c b t"), xnf1[:, :, :]).then_inc(stored, 16)

            program("sp", sp, step)
            sp.wait_ge(stored, 16 * NP)

        @block.tensor
        def _(pe):
            def mm(o, l, r, start=True, stop=True):
                return nc.tensor.matmul(o, l, r, start=start, stop=stop, skip_group_check=True)

            def step(name, p, k):
                if name == "query0":
                    pe.wait_ge(ld_w, 16 * 8)
                    pe.wait_ge(ln[0], 8 * (p + 1))
                    if due(p - 1):
                        pe.wait_ge(v1c, p - 1)
                    if due(p):
                        pe.wait_ge(cl[0], p)
                    mm(pa[:, :], wq[:, :], xn0[:, :, :].rearrange("p b t -> p (b t)")).then_inc(s_qp, 1)
                elif name == "key0":
                    pe.wait_ge(ld_in, 64 * (p + 1))
                    pe.wait_ge(s_qf, p + 1)
                    mm(pa[:, :], wk[:, :], ctx0[:, :, :].rearrange("p b t -> p (b t)")).then_inc(s_kp, 1)
                elif name == "value0":
                    pe.wait_ge(s_kf, p + 1)
                    for b in range(NB):
                        for s in range(2):
                            j = 2 * b + s
                            last = mm(pa[:, 128 * j:128 * j + 128], ctx0[:, b, 128 * s:128 * s + 128], wv[:, :])
                    last.then_inc(s_vp, 1)
                elif name == "values1":
                    pe.wait_ge(ld_c1, 16 * (p + 1))
                    pe.wait_ge(cl[0], lim(p + 2))
                    for b in range(NB):
                        for s in range(2):
                            j = 2 * b + s
                            last = nc.tensor.transpose(pa[:, 128 * j:128 * j + 128],
                                                       ctx1[:, b, 128 * s:128 * s + 128], ident[:, :])
                    last.then_inc(v1p, 1)
                elif name in ("max0", "max1"):
                    i, L = layer(name)
                    h, b, g = max_unit(L, k)
                    if k % (2 * L.NG) == 0:
                        pe.wait_ge(ka[i][g], 48 * (p + 1))
                    if k == 0:
                        pe.wait_ge(qa[i], 48 * (p + 1))
                        if i == 0:
                            pe.wait_ge(ma[0], 32 * (p + 1))
                        pe.wait_ge(set_o, 16 * (L0.HPG + L1.HPG))
                        if i == 0:
                            if due(L1.U * (p - 1)):
                                pe.wait_ge(md[1], L1.U * (p - 1))
                            if due(L0.U * p):
                                pe.wait_ge(md[0], L0.U * p)
                        else:
                            pe.wait_ge(md[0], L0.U * lim(p + 2))
                    elif k >= 2:
                        if due(L.U * p + k - 1):
                            pe.wait_ge(md[i], L.U * p + k - 1)
                    for s in range(2):
                        q0 = b * T + 128 * s
                        last = mm(mxp[k % 2][:, T * s:T * s + T], QT[i][0:L.SHIFT, h // L.HPG, q0:q0 + 128],
                                  KM[i][0:L.SHIFT, h, b * T:b * T + T])
                    last.then_inc(mp[i], 1)
                elif name in ("turnmax0", "turnmax1"):
                    i, L = layer(name)
                    pe.wait_ge(md[i], L.U * (p + 1))
                    if i == 0:
                        if due(p - 1):
                            pe.wait_ge(cl[1], p - 1)
                        pe.wait_ge(s_vf, p + 1)
                    else:
                        pe.wait_ge(s_vf, lim(p + 3))
                        pe.wait_ge(v1c, p + 1)
                    for b in range(NB):
                        for s in range(2):
                            j = 2 * b + s
                            last = mm(pa[0:L.H, 128 * j:128 * j + 128], mx[:, b, s, 0:L.H], ident[:, :])
                    last.then_inc(cp[i], 1)
                elif name in ("exp0", "exp1"):
                    i, L = layer(name)
                    if k == 0:
                        pe.wait_ge(cd[i], 16 * (p + 1))
                        if i == 0:
                            if due(L1.U * (p - 1)):
                                pe.wait_ge(ex[1], L1.U * (p - 1))
                            if due(L0.U * p):
                                pe.wait_ge(ex[0], L0.U * p)
                        else:
                            pe.wait_ge(ex[0], L0.U * lim(p + 2))
                    if k >= 3:
                        if due(L.U * p + k - 2):
                            pe.wait_ge(ex[i], L.U * p + k - 2)
                    h, b = unit(k)
                    for s in range(2):
                        k0 = b * T + 128 * s
                        last = mm(exq[(k + 2 * i) % 3][:, T * s:T * s + T], KM[i][0:L.KE, h, k0:k0 + 128],
                                  QT[i][0:L.KE, h // L.HPG, b * T:b * T + T])
                    last.then_inc(sc[i], 1)
                elif name in ("pv0", "pv1"):
                    i, L = layer(name)
                    pe.wait_ge(ex[i], L.U * p + 4 * k + 4)
                    if k == 0:
                        pe.wait_ge((plv, v1c)[i], p + 1)
                        if i == 0:
                            if due(L1.NT * (p - 1)):
                                pe.wait_ge(og[1], L1.NT * (p - 1))
                            if due(L0.NT * p):
                                pe.wait_ge(og[0], L0.NT * p)
                        else:
                            pe.wait_ge(og[0], L0.NT * lim(p + 2))
                    elif k % 2 == 0:
                        if due(L.NT * p + k // 2):
                            pe.wait_ge(og[i], L.NT * p + k // 2)
                    b = k % 2
                    for s in range(2):
                        for g in range(4):
                            h = 4 * (k // 2) + g
                            last = mm(pv[32 * g:32 * g + 32, b * T:b * T + T], V[i][:, 2 * b + s, h, :],
                                      P[:, (4 * k + g) % PR, T * s:T * s + T], start=s == 0, stop=s == 1)
                    last.then_inc(pvd[i], 1)
                elif name == "rank":
                    pe.wait_ge(rt, 12 * p + 6)
                    if due(p - 1):
                        pe.wait_ge(x4c, p - 1)
                    if due(p):
                        pe.wait_ge(x2c, p)
                    for b in range(NB):
                        last = nc.tensor.transpose(pf[:, 128 * b:128 * b + 128], sbc[:, b, :], ident[:, :])
                    last.then_inc(rtp, 1)
                elif name == "pick":
                    if due(12 * p + 12):
                        pe.wait_ge(rt, 12 * p + 12)
                    for d in range(2):
                        for b in range(NB):
                            o = 128 * d + KEEP * b
                            mm(pf[:, o:o + KEEP], xnf0[:, b, 128 * d:128 * d + 128], oh[:, b, :])
                    nc.tensor.transpose(pf[:, 256:384], oh[:, :, :].rearrange("p b k -> p (b k)"), ident[:, :]).then_inc(xsp, 1)
                elif name == "up2":
                    if k == 0:
                        pe.wait_ge(ld_m, 16 * 4)
                        pe.wait_ge(xsc, 2 * (p + 1))
                    else:
                        pe.wait_ge(hz, 2 * p + 1)
                    for f in range(4):
                        for d in range(2):
                            c0 = 128 * (4 * k + f)
                            last = mm(pf[:, 128 * f:128 * f + 128], w1[:, d, c0:c0 + 128], xsT[:, d, :],
                                      start=d == 0, stop=d == 1)
                    last.then_inc(hp, 1)
                elif name == "down2":
                    pe.wait_ge(g_h, p + 1)
                    for f in range(FC):
                        last = mm(pf[:, 0:T], z[:, 128 * f:128 * f + 128], w2[:, f, :], start=f == 0, stop=f == FC - 1)
                    last.then_inc(yp, 1)
                elif name == "spread":
                    pe.wait_ge(yc, p + 1)
                    mm(pf[:, 0:T], ohT[0:KEEP, :], y0[0:KEEP, :]).then_inc(x2q, 1)
                    pe.wait_ge(x2q, p + 1)
                    mm(pf[:, T:2 * T], ohT[KEEP:2 * KEEP, :], y0[KEEP:2 * KEEP, :]).then_inc(x2p, 1)
                elif name == "turn3":
                    pe.wait_ge(ln[3], 8 * (p + 1))
                    pe.wait_ge(x2c, lim(p + 2))
                    for d in range(2):
                        for b in range(NB):
                            o = T * d + 128 * b
                            last = nc.tensor.transpose(pf[:, o:o + 128], xnf1[:, b, 128 * d:128 * d + 128], ident[:, :])
                    last.then_inc(xtp, 1)
                elif name == "up3":
                    if k == 0:
                        pe.wait_ge(xtc, p + 1)
                        pe.wait_ge(lku, LKN)
                    else:
                        if due(OC * p + k):
                            pe.wait_ge(s_h1, OC * p + k)
                    for w, o in ((wg, 0), (wu, T)):
                        for d in range(2):
                            last = mm(pf[0:OM[k], o:o + T], w[:, d, 128 * k:128 * k + OM[k]], xT[:, d, :],
                                      start=d == 0, stop=d == 1)
                    last.then_inc(gup, 1)
                elif name == "down3":
                    pe.wait_ge(s_h1, OC * (p + 1))
                    for b in range(NB):
                        for o in range(OC):
                            last = mm(pf[:, T * b:T * b + T], h1[0:OM[o], o, 128 * b:128 * b + 128],
                                      wd[0:OM[o], o, :], start=o == 0, stop=o == OC - 1)
                    last.then_inc(dnp, 1)

            program("pe", pe, step)

        @block.scalar
        def _(act):
            act.wait_ge(ld_w, 16 * 8)
            nc.scalar.activation(tg[:, :], gts[:, 0:4], ACT.Tanh).then_inc(s_tg, 1)

            def step(name, p, k):
                if name in ("query0b", "key0b"):
                    dst, prod_, done, j = ((qf, s_qp, s_qf, 0), (kf, s_kp, s_kf, 1))[name == "key0b"]
                    act.wait_ge(prod_, p + 1)
                    if due(6 * p):
                        act.wait_ge(pl0, 6 * p)
                    nc.scalar.activation(dst[:, :], pa[:, :], ACT.Identity, bias=bqk[:, j:j + 1]).then_inc(done, 1)
                elif name == "values1b":
                    act.wait_ge(v1p, p + 1)
                    if due(L1.U // 4 * p):
                        act.wait_ge(pvd[1], L1.U // 4 * p)
                    act.wait_ge(set_z, 5)
                    nc.scalar.copy(V[1][:, :, :, 0:L1.DH],
                                   pa[:, :].rearrange("p (j h d) -> p j h d", j=4, h=L1.H)).then_inc(v1c, 1)
                elif name in ("shift0", "shift1"):
                    i, L = layer(name)
                    act.wait_ge(cp[i], p + 1)
                    if i == 0:
                        if due(p - 1):
                            act.wait_ge(cw[1], 32 * (p - 1))
                        if due(p):
                            act.wait_ge(cw[0], 32 * p)
                    else:
                        act.wait_ge(cw[0], 32 * lim(p + 2))
                    nc.scalar.activation(chi[0:L.H, :], pa[0:L.H, :], ACT.Copy, scale=-1.0).then_inc(ch[i], 1)
                elif name in ("exp0", "exp1"):
                    i, L = layer(name)
                    act.wait_ge(sc[i], L.U * p + k + 1)
                    if k % 4 == 0:
                        if k >= PR:
                            act.wait_ge(pvd[i], L.U // 4 * p + (k - PR) // 4 + 1)
                        elif i == 0:
                            if due(L1.U // 4 * (p - 1)):
                                act.wait_ge(pvd[1], L1.U // 4 * (p - 1))
                            if due(L0.U // 4 * p):
                                act.wait_ge(pvd[0], L0.U // 4 * p)
                        else:
                            act.wait_ge(pvd[0], L0.U // 4 * lim(p + 2))
                    nc.scalar.activation(P[:, k % PR, :], exq[(k + 2 * i) % 3][:, :], ACT.Exp,
                                         scale=L.scale).then_inc(ex[i], 1)
                elif name in ("out0", "out1"):
                    i, L = layer(name)
                    act.wait_ge(pvd[i], L.U // 4 * p + 2 * k + 2)
                    if k >= 2:
                        if due(128 * (2 * p + 1)):
                            act.wait_ge(ow[i][k % 2], 16 * (2 * p + 1))
                    elif i == 0:
                        if due(p - 1):
                            act.wait_ge(ow[1][k % 2], 16 * (p - 1))
                        if due(p):
                            act.wait_ge(ow[0][k % 2], 32 * p)
                    else:
                        if due(128 * 2 * lim(p + 2)):
                            act.wait_ge(ow[0][k % 2], 32 * lim(p + 2))
                    nc.scalar.copy(OG[:, k % 2, :], pv[:, :]).then_inc(og[i], 1)
                elif name == "picked":
                    act.wait_ge(xsp, p + 1)
                    if due(2 * p):
                        act.wait_ge(hp, 2 * p)
                    if due(p):
                        act.wait_ge(x2p, p)
                    nc.scalar.copy(xsT[:, :, :].rearrange("p d k -> p (d k)"), pf[:, 0:256]).then_inc(xsc, 1)
                    nc.scalar.copy(ohT[:, :], pf[:, 256:384]).then_inc(xsc, 1)
                elif name == "square2":
                    act.wait_ge(hz, 2 * (p + 1))
                    nc.scalar.activation(gz[:, :], z[:, :], ACT.Square).then_inc(g_sq, 1)
                elif name == "tanh2":
                    act.wait_ge(g_in, 2 * (p + 1))
                    nc.scalar.activation(gz[:, :], gz[:, :], ACT.Tanh, scale=GELU_C).then_inc(g_th, 1)
                elif name == "turned3":
                    act.wait_ge(xtp, p + 1)
                    if due(OC * p):
                        act.wait_ge(gup, OC * p)
                    act.wait_ge(lku, LKN)
                    nc.scalar.copy(xT[:, :, :].rearrange("p d n -> p (d n)"), pf[:, :]).then_inc(xtc, 1)
                elif name == "tanh3":
                    act.wait_ge(gup, OC * p + k + 1)
                    if due(OC * p + max(k - 1, 0)):
                        act.wait_ge(s_ga, OC * p + max(k - 1, 0))
                    nc.scalar.activation(th[0:OM[k], k % 2, :], pf[0:OM[k], 0:T], ACT.Tanh, scale=0.5).then_inc(s_th, 1)

            program("act", act, step)

        @block.vector
        def _(dve):
            def stats(i, x, p):
                n0 = 8 * p
                if due(n0):
                    dve.wait_ge(ln[i], n0)
                for b in range(NB):
                    nc.vector.bn_stats(stat[i][:, b, :], x[:, b, :]).then_inc(ln[i], 1)
                dve.wait_ge(ln[i], n0 + 2)
                settle(dve, passed_dve)
                for b in range(NB):
                    nc.vector.bn_aggr(mv[i][:, b, :], stat[i][:, b, :]).then_inc(ln[i], 1)
                dve.wait_ge(ln[i], n0 + 4)
                nc.vector.tensor_scalar(rstd[i][:, :], mv[i][:, :, 1], EPS, None, ALU.add).then_inc(ln[i], 1)

            def scale(i, x, xn, p):
                dve.wait_ge(ln[i], 8 * p + 6)
                for b in range(NB):
                    nc.vector.tensor_scalar(xn[:, b, :], x[:, b, :], mv[i][:, b, 0:1], rstd[i][:, b:b + 1],
                                            ALU.subtract, ALU.mult).then_inc(ln[i], 1)

            def lookup(c):
                w, c0, n = lookup_chunk(c)
                idx = w[:, c0:c0 + n].bitcast(U32)
                at = [LKC * c]

                def do(ins):
                    ins.then_inc(lku, 1)
                    at[0] += 1
                    dve.wait_ge(lku, at[0])

                m0, m1, m2, m3, t1, t2, t3 = (x[:, 0:n] for x in lk)
                do(nc.vector.tensor_scalar(m0.bitcast(I32), idx.bitcast(I32), 31, 31, ALU.logical_shift_left, ALU.arith_shift_right))
                for m, bit in ((m1, 2), (m2, 4), (m3, 8)):
                    do(nc.vector.tensor_scalar(m, idx, bit, None, ALU.bitwise_and))

                def leaf(dst, j):
                    do(nc.vector.tensor_scalar(dst, m0, lutx[:, j:j + 1], lut[:, 2 * j:2 * j + 1],
                                               ALU.bitwise_and, ALU.bitwise_xor))

                def four(dst, tmp, j):
                    leaf(dst, 2 * j)
                    leaf(tmp, 2 * j + 1)
                    do(nc.vector.copy_predicated(dst, m1, tmp))

                four(idx, t1, 0)
                four(t2, t1, 1)
                do(nc.vector.copy_predicated(idx, m2, t2))
                four(t2, t1, 2)
                four(t3, t1, 3)
                do(nc.vector.copy_predicated(t2, m2, t3))
                do(nc.vector.copy_predicated(idx, m3, t2))
                assert at[0] == LKC * (c + 1)

            nc.vector.memset(f32(KM[0][:, :, :]), 0.0).then_inc(set_z, 1)
            nc.vector.memset(ones[:, :], 1.0).then_inc(set_z, 1)
            nc.vector.memset(f32(KM[1][:, :, :]), 0.0).then_inc(set_z, 1)
            dve.wait_ge(s_tg, 1)
            nc.vector.tensor_tensor(tgx[:, 0:1], tg[:, 2:3], gts[:, 4:5], ALU.mult).then_inc(s_tg, 1)
            nc.vector.tensor_scalar(tgx[:, 1:2], tg[:, 3:4], 0.5, None, ALU.mult).then_inc(s_tg, 1)
            dve.wait_ge(ld_b, 16 * 5)
            lv = lut[:, :].rearrange("p (j two) -> p j two", two=2)
            nc.vector.tensor_tensor(lutx[:, :], lv[:, :, 0], lv[:, :, 1], ALU.bitwise_xor).then_inc(s_tg, 1)
            dve.wait_ge(s_tg, 4)
            dve.wait_ge(ld_i, 16 * 3)

            def flat(t):
                return t[:, :, :].rearrange("p b t -> p (b t)")

            def step(name, p, k):
                if name == "stats0":
                    dve.wait_ge(ld_in, 64 * (p + 1))
                    stats(0, xin, p)
                elif name == "scale0":
                    if due(p):
                        dve.wait_ge(s_qp, p)
                    scale(0, xin, xn0, p)
                elif name == "stats1":
                    dve.wait_ge(x2c, p + 1)
                    stats(2, x2, p)
                elif name == "scale1":
                    if due(p):
                        dve.wait_ge(pl1, 4 * p)
                    scale(2, x2, xn1, p)
                elif name == "stats3":
                    dve.wait_ge(xo[1], p + 1)
                    stats(3, x3, p)
                elif name == "scale3":
                    if due(p):
                        dve.wait_ge(stored, 16 * p)
                    scale(3, x3, xnf1, p)
                elif name == "lookup":
                    lookup(k)
                elif name == "masks0":
                    if due(p):
                        dve.wait_ge(ma[0], 32 * p)
                    m = mrA[:, :, :].rearrange("p b t -> p (b t)")
                    nc.vector.tensor_scalar(mt[:, :], m[0:2, :], 1.0, None, ALU.mult).then_inc(pm, 1)
                    nc.vector.tensor_scalar(ng[:, :], m[0:2, :], -1.0, negs[:, 0:1], ALU.add, ALU.mult).then_inc(pm, 1)
                elif name == "value0b":
                    dve.wait_ge(s_vp, p + 1)
                    if due(p):
                        dve.wait_ge(plv, p)
                    nc.vector.tensor_tensor(vf[:, :].rearrange("p (j n) -> p j n", j=4),
                                            pa[:, :].rearrange("p (j n) -> p j n", j=4),
                                            bv[:, :].unsqueeze(1).to_broadcast([128, 4, 128]), ALU.add).then_inc(s_vf, 1)
                elif name in ("max0", "max1"):
                    i, L = layer(name)
                    dve.wait_ge(mp[i], L.U * p + k + 1)
                    if k == 0 and i == 0:
                        if due(p - 1):
                            dve.wait_ge(cp[1], p - 1)
                        if due(p):
                            dve.wait_ge(cp[0], p)
                    if k == 0 and i == 1:
                        dve.wait_ge(cp[0], lim(p + 2))
                    h, b, _ = max_unit(L, k)
                    nc.vector.tensor_reduce(mx[:, b, :, h], mxp[k % 2][:, :].rearrange("p (s t) -> p s t", s=2),
                                            AX.X, ALU.max).then_inc(md[i], 1)
                elif name in ("shift0", "shift1"):
                    i, L = layer(name)
                    dve.wait_ge(ch[i], p + 1)
                    nc.vector.scalar_tensor_tensor(out=clo[0:L.H, :], in0=pa[0:L.H, :], scalar=-1.0,
                                                   in1=f32(chi[0:L.H, :]), op0=ALU.mult,
                                                   op1=ALU.subtract).then_inc(cl[i], 1)
                elif name in ("resid0", "resid1"):
                    i, L = layer(name)
                    dve.wait_ge(ocr[i], 16 * (p + 1))
                    dve.wait_ge(dcr[i], 16 * (p + 1))
                    nc.vector.tensor_tensor(Oc[:, :], Oc[:, :], Dc[:, :], ALU.mult).then_inc(dv[i], 1)
                    if i == 1:
                        dve.wait_ge(dv[1], p + 1)
                        if due(p):
                            dve.wait_ge(x4c, p)
                        nc.vector.scalar_tensor_tensor(out=flat(x3), in0=Oc[:, :], scalar=tgx[:, 0:1], in1=flat(x2),
                                                       op0=ALU.mult, op1=ALU.add).then_inc(xo[1], 1)
                elif name == "skip0":
                    dve.wait_ge(om[0], p + 1)
                    dve.wait_ge(xcp, p + 1)
                    if due(p):
                        dve.wait_ge(x2c, p)
                    dve.wait_ge(s_tg, 4)
                    nc.vector.scalar_tensor_tensor(out=flat(x1), in0=Oc[:, :], scalar=tg[:, 0:1], in1=flat(xr0),
                                                   op0=ALU.mult, op1=ALU.add).then_inc(xo[0], 1)
                elif name in ("invert0", "invert1"):
                    i, L = layer(name)
                    dve.wait_ge(dr[i], 16 * (p + 1))
                    w = L.H * N // 128
                    nc.vector.reciprocal(Dn[:, 0:w], Dn[:, 0:w]).then_inc(rc[i], 1)
                elif name == "stats2":
                    dve.wait_ge(xo[0], p + 1)
                    stats(1, x1, p)
                elif name == "scale2":
                    if due(p):
                        dve.wait_ge(xsp, p)
                    scale(1, x1, xnf0, p)
                    dve.wait_ge(ln[1], 8 * (p + 1))
                    if due(p):
                        dve.wait_ge(rtp, p)
                    if due(12 * p):
                        dve.wait_ge(rt, 12 * p)
                    for b in range(NB):
                        if due(12 * p + b):
                            dve.wait_ge(rt, 12 * p + b)
                        settle(dve, passed_dve)
                        nc.vector.tensor_tensor_reduce(prod[:, :], xnf0[:, b, :], wr[:, :], 1.0, 0.0, ALU.mult,
                                                       ALU.add, rs[:, b, 0:1]).then_inc(rt, 1)
                    dve.wait_ge(rt, 12 * p + 2)
                    for b in range(NB):
                        nc.vector.tensor_scalar(rs[:, b, 1:2], rs[:, b, 0:1], br[:, 0:1], None, ALU.add).then_inc(rt, 1)
                    dve.wait_ge(rt, 12 * p + 4)
                    for b in range(NB):
                        nc.vector.tensor_scalar(sbc[:, b, :], tril[:, :], 0.0, rs[:, b, 1:2], ALU.mult,
                                                ALU.add).then_inc(rt, 1)
                elif name == "onehot":
                    dve.wait_ge(rtp, p + 1)
                    if due(p):
                        dve.wait_ge(xsp, p)
                    for b in range(NB):
                        row = pf[:, 128 * b:128 * b + 128]
                        nc.vector.tensor_scalar(prod[:, 0:128], row, rs[:, b, 1:2], None, ALU.is_gt).then_inc(rt, 1)
                        nc.vector.scalar_tensor_tensor(out=prod[:, 128:256], in0=row, scalar=rs[:, b, 1:2],
                                                       in1=tril[:, :], op0=ALU.is_equal, op1=ALU.mult).then_inc(rr, 1)
                        dve.wait_ge(rr, 2 * p + b + 1)
                        dve.wait_ge(rt, 12 * p + 7 + 3 * b)
                        settle(dve, passed_dve)
                        nc.vector.tensor_tensor_reduce(prod[:, 0:128], prod[:, 0:128], prod[:, 128:256], 1.0, 0.0,
                                                       ALU.add, ALU.add, rs[:, b, 2:3]).then_inc(rt, 1)
                        dve.wait_ge(rt, 12 * p + 8 + 3 * b)
                        nc.vector.tensor_scalar(oh[:, b, :], iota[:, :], rs[:, b, 2:3], None, ALU.is_equal).then_inc(rt, 1)
                elif name == "bias2":
                    dve.wait_ge(hp, 2 * p + k + 1)
                    if due(p):
                        dve.wait_ge(yp, p)
                    nc.vector.tensor_tensor(z[:, 512 * k:512 * k + 512].rearrange("p (f n) -> p f n", f=4),
                                            pf[:, :].rearrange("p (f n) -> p f n", f=4),
                                            b1[:, 4 * k:4 * k + 4].unsqueeze(2).to_broadcast([128, 4, 128]),
                                            ALU.add).then_inc(hz, 1)
                elif name == "gelu2":
                    dve.wait_ge(g_th, p + 1)
                    nc.vector.scalar_tensor_tensor(out=z[:, :], in0=gz[:, :], scalar=1.0, in1=z[:, :],
                                                   op0=ALU.add, op1=ALU.mult).then_inc(g_h, 1)
                elif name == "half2":
                    dve.wait_ge(yp, p + 1)
                    if due(p):
                        dve.wait_ge(x2p, p)
                    nc.vector.scalar_tensor_tensor(out=y0[:, :], in0=pf[:, 0:T], scalar=0.5, in1=b2[:, :],
                                                   op0=ALU.mult, op1=ALU.add).then_inc(yc, 1)
                elif name == "add2":
                    dve.wait_ge(x2p, p + 1)
                    if due(p):
                        dve.wait_ge(xo[1], p)
                    nc.vector.scalar_tensor_tensor(out=x2[:, :, :], in0=pf[:, :].rearrange("p (b t) -> p b t", b=NB),
                                                   scalar=tg[:, 1:2], in1=x1[:, :, :],
                                                   op0=ALU.mult, op1=ALU.add).then_inc(x2c, 1)
                elif name == "hidden3":
                    m = OM[k]
                    dve.wait_ge(s_th, OC * p + k + 1)
                    if due(OC * p + k):
                        dve.wait_ge(s_h1, OC * p + k)
                    nc.vector.scalar_tensor_tensor(out=ga1[0:m, :], in0=th[0:m, k % 2, :], scalar=1.0,
                                                   in1=pf[0:m, 0:T], op0=ALU.add, op1=ALU.mult).then_inc(s_ga, 1)
                    dve.wait_ge(s_ga, OC * p + k + 1)
                    if due(p):
                        dve.wait_ge(dnp, p)
                    nc.vector.tensor_tensor(h1[0:m, k, :], ga1[0:m, :], pf[0:m, T:2 * T], ALU.mult).then_inc(s_h1, 1)
                elif name == "add3":
                    dve.wait_ge(dnp, p + 1)
                    nc.vector.scalar_tensor_tensor(out=xnf1[:, :, :], in0=pf[:, :].rearrange("p (b t) -> p b t", b=NB),
                                                   scalar=tgx[:, 1:2], in1=x3[:, :, :],
                                                   op0=ALU.mult, op1=ALU.add).then_inc(x4c, 1)

            program("dve", dve, step)

        @block.gpsimd
        def _(pool):
            for i, L in enumerate((L0, L1)):
                nc.gpsimd.memset(V[i][:, :, :, L.DH:32], 0.0).then_inc(set_v, 1)
            nc.gpsimd.memset(mhalf[:, :], -0.5).then_inc(set_v, 1)
            pool.wait_ge(set_v, 3)
            for i, L in enumerate((L0, L1)):
                nc.gpsimd.memset(V[i][:, :, :, L.DH:2 * L.DH], 1.0).then_inc(set_z, 1)

            def split(src, hi, lo, sm, n):
                settle(pool, passed_pool)
                nc.gpsimd.tensor_scalar(hi, src, 1.0, None, ALU.mult).then_inc(sm, 1)
                if due(n):
                    pool.wait_ge(sm, n)
                nc.gpsimd.tensor_tensor(lo, src, f32(hi), ALU.subtract).then_inc(sm, 1)

            def step(name, p, k):
                flat = lambda t: t[:, :, :].rearrange("p b t -> p (b t)")
                if name in ("stats0", "stats1", "stats2", "stats3"):
                    i = {"stats0": 0, "stats2": 1, "stats1": 2, "stats3": 3}[name]
                    pool.wait_ge(ln[i], 8 * p + 5)
                    nc.gpsimd.tensor_tensor(rstd[i][:, :], rstd[i][:, :], mhalf[:, :], ALU.pow).then_inc(ln[i], 1)
                elif name == "split0":
                    pool.wait_ge(ld_in, 64 * (p + 1))
                    for stored_parts in (qw, kw):
                        if due(p):
                            pool.wait_ge(stored_parts[0], 16 * p)
                        if due(p - 1):
                            pool.wait_ge(stored_parts[1], 16 * (p - 1))
                    m = flat(mrA)
                    for j, (t, done, hi, lo) in enumerate(((qf, s_qf, qhl[:, 0, :], qhl[:, 1, :]), (kf, s_kf, khl[:, 0, :], khl[:, 1, :]))):
                        pool.wait_ge(done, p + 1)
                        nc.gpsimd.tensor_tensor(t[:, :], t[:, :], m, ALU.mult).then_inc(pl0, 1)
                        pool.wait_ge(pl0, 6 * p + 3 * j + 1)
                        split(t[:, :], hi, lo, pl0, 6 * p + 3 * j + 2)
                elif name == "values0":
                    pool.wait_ge(s_vf, p + 1)
                    if due(L0.U // 4 * p):
                        pool.wait_ge(pvd[0], L0.U // 4 * p)
                    nc.gpsimd.tensor_tensor(V[0][:, :, :, 0:L0.DH], vf[:, :].rearrange("p (j h d) -> p j h d", j=4, h=L0.H),
                                            mc[:, :].unsqueeze(2).unsqueeze(3).to_broadcast([128, 4, L0.H, L0.DH]),
                                            ALU.mult).then_inc(plv, 1)
                elif name == "split1":
                    pool.wait_ge(ln[2], 8 * (p + 1))
                    pool.wait_ge(ld_c1, 16 * (p + 1))
                    for stored_parts in (qw, kw):
                        pool.wait_ge(stored_parts[0], 16 * lim(p + 2))
                    split(flat(xn1), qhl[:, 0, :], qhl[:, 1, :], pl1, 4 * p + 1)
                    split(flat(ctx1), khl[:, 0, :], khl[:, 1, :], pl1, 4 * p + 3)
                elif name == "keep0":
                    pool.wait_ge(ln[0], 8 * (p + 1))
                    if due(p):
                        pool.wait_ge(xo[0], p)
                    settle(pool, passed_pool)
                    nc.gpsimd.tensor_scalar(flat(xr0), flat(xin), 1.0, None, ALU.mult).then_inc(xcp, 1)
                elif name == "resid0":
                    pool.wait_ge(dv[0], p + 1)
                    pool.wait_ge(ld_mb, 16 * (p + 1))
                    nc.gpsimd.tensor_tensor(Oc[:, :], Oc[:, :], flat(mrB), ALU.mult).then_inc(om[0], 1)
                elif name == "inner2":
                    pool.wait_ge(g_sq, p + 1)
                    settle(pool, passed_pool)
                    nc.gpsimd.tensor_scalar(gz[:, :], gz[:, :], 0.044715, 1.0, ALU.mult, ALU.add).then_inc(g_in, 1)
                    pool.wait_ge(g_in, 2 * p + 1)
                    nc.gpsimd.tensor_tensor(gz[:, :], gz[:, :], z[:, :], ALU.mult).then_inc(g_in, 1)

            program("pool", pool, step)


def kernel(**inputs):
    import numpy as _np
    import concourse.bacc as _bacc
    from concourse import mybir as _mybir
    from concourse.bass_utils import run_bass_kernel_spmd as _run

    v = {k: _np.asarray(x) for k, x in inputs.items()}
    chunks = lambda w, n: _np.pad(w, ((0, n * 128 - w.shape[0]), (0, 0))).reshape(n, 128, -1).transpose(1, 0, 2)
    laid = {
        "x": v["x"], "ctx_2048": v["ctx_2048"],
        "wqT": v["L0_xattn_Wq"].T, "wkT": v["L0_xattn_Wk"].T, "wvT": v["L0_xattn_Wv"].T,
        "bqk": _np.stack([v["L0_xattn_bq"], v["L0_xattn_bk"]], 1), "L0_xattn_bv": v["L0_xattn_bv"],
        "gts": _np.stack([v["g_xattn"][0], v["g_ffn"][0], v["g_xattn"][1], v["g_ffn"][1],
                          v["L1_xattn_gamma"]]).reshape(1, 5),
        "mrow": v["mask_Bx1x2048_fk1"].reshape(NP, N),
        "mcol": v["mask_Bx1x2048_fk1"].reshape(NP, NB * 2, 128).transpose(0, 2, 1),
        "L0_ffn_w_r": v["L0_ffn_w_r"], "br": v["L0_ffn_b_r"].reshape(1, 1),
        "L0_ffn_w1": v["L0_ffn_w1"], "b1c": v["L0_ffn_b1"].reshape(FC, 128).T,
        "L0_ffn_w2": v["L0_ffn_w2"], "L0_ffn_b2": v["L0_ffn_b2"],
        "L1_ffn_lut": v["L1_ffn_lut"],
        "gate_i": chunks(v["L1_ffn_gate_idx"].T, 2), "up_i": chunks(v["L1_ffn_up_idx"].T, 2),
        "down_i": chunks(v["L1_ffn_down_idx"].T, OC),
        "negs": _np.array([[NEG_HI], [NEG_LO]], _np.float32),
        "ident": _np.eye(128, dtype=_np.float32), "tril": _np.tril(_np.ones((128, 128), _np.float32), -1),
        "iota": _np.arange(KEEP, dtype=_np.float32).reshape(1, KEEP),
    }
    nc = _bacc.Bacc("TRN2", target_bir_lowering=False, num_devices=1)
    arrays, aps = {}, {}
    for name, x in laid.items():
        x = _np.ascontiguousarray(x)
        arrays[f"in_{name}"] = x
        aps[name] = nc.dram_tensor(f"in_{name}", x.shape, _mybir.dt.from_np(x.dtype), kind="ExternalInput").ap()
    out = nc.dram_tensor("out", (B, C, T), _mybir.dt.from_np(_np.dtype("float32")), kind="ExternalOutput").ap()
    flamingo_kernel(nc, aps, out)
    r = _run(nc, [arrays], core_ids=[0])
    return r.results[0]["out"]
```

```python
from contextlib import ExitStack

import numpy as np

import concourse.bass as bass
from concourse import mybir

F32 = mybir.dt.float32
F32R = mybir.dt.float32r
I32 = mybir.dt.int32
U32 = mybir.dt.uint32
ALU = mybir.AluOpType
ACT = mybir.ActivationFunctionType
AX = mybir.AxisListType

B, C, T = 16, 128, 256
NB = 2
NP = B // NB
N = NB * T
DF, FC = 1024, 8
INTER, OC = 688, 6
OM = [min(128, INTER - 128 * o) for o in range(OC)]
KEEP = 64
LUT = 16
EPS = 1e-5
NEG = 1e6
GELU_C = float(np.sqrt(2.0 / np.pi))


class Layer:

    def __init__(self, heads, masked):
        self.H = heads
        self.DH = 128 // heads
        self.HPG = 32 // self.DH
        self.NG = 4
        self.SHIFT = 98 if masked else 96
        self.KE = self.SHIFT + 2 * self.HPG
        self.U = heads * NB
        self.NT = heads // 4
        self.scale = 1.0 / float(np.sqrt(self.DH))


L0 = Layer(16, True)
L1 = Layer(8, False)
NEG0 = NEG / L0.scale
NEG_HI = float(np.round(NEG0 / 2048) * 2048)
NEG_LO = NEG0 - NEG_HI


PAIR = {"n0": 1, "a0": 1, "m0": 0, "e0": 0, "o0": -1, "f0": -1, "m1": -1, "e1": -2, "f1": -2}

STEPS = (
    ("exp0", "e0", L0.U, -0.1, 1.006),
    ("max1", "m1", L1.U, 12.62, 1.021),
    ("pv0", "e0", L0.U // 4 - 1, 6.05, 4.21),
    ("out0", "e0", L0.NT - 1, 10.35, 8.124),
    ("stats1", "m1", 1, -2.26, 0), ("stats3", "f1", 1, 0.5, 0), ("scale1", "m1", 1, 1.66, 0), ("load", "n0", 1, -26.91, 0),
    ("scale3", "f1", 1, 2.52, 0), ("split1", "m1", 1, 3.05, 0), ("turn3", "f1", 1, 3.23, 0), ("store1", "m1", 1, 0.59, 0),
    ("turned3", "f1", 1, 3.78, 0), ("values1", "m1", 1, 2.42, 0), ("values1b", "m1", 1, 13.68, 0),
    ("assemble1", "m1", 1, 1.93, 0), ("keys1", "m1", L1.HPG, 4.54, 0.104),
    ("stats0", "n0", 1, -23.73, 0), ("scale0", "n0", 1, -19.57, 0), ("masks0", "n0", 1, -8.27, 0),
    ("query0", "n0", 1, -18.29, 0), ("query0b", "n0", 1, -14.09, 0), ("key0", "n0", 1, -15.97, 0), ("key0b", "n0", 1, -10.13, 0),
    ("value0", "n0", 1, -13.15, 0), ("split0", "n0", 1, -8.3, 0), ("value0b", "n0", 1, -8.86, 0),
    ("store0", "n0", 1, 0.09, 0), ("turnmax1", "m1", 1, 29.2, 0), ("shift1", "m1", 1, 29.13, 0),
    ("up3", "f1", OC, 5.62, 3.69), ("tanh3", "f1", OC, 6.79, 3.128), ("hidden3", "f1", OC, 6.24, 3.869),
    ("assemble0", "a0", 1, -0.08, 0), ("keys0", "a0", L0.HPG, 15.24, 7.72),
    ("pv0last", "e0", 1, 31.9, 0), ("out0last", "e0", 1, 33.72, 0), ("down3", "f1", 1, 32.16, 0),
    ("gather0", "e0", 1, 35.0, 0), ("values0", "a0", 1, 31.68, 0), ("invert0", "o0", 1, -41.5, 0), ("add3", "f1", 1, 39.8, 0),
    ("exp1", "e1", 4, -42.1, 0.072), ("exp1more", "e1", L1.U - 4, -39.67, 1.403),
    ("max0", "a0", 8, 30.7, 0.779), ("max0more", "m0", L0.U - 8, -41.3, 1.2),
    ("pv1", "e1", L1.U // 4 - 1, -36.3, 5.506), ("out1", "e1", 1, -33.51, 0),
    ("pv1last", "e1", 1, -18.36, 0), ("out1last", "e1", 1, -17.06, 0), ("gather1", "e1", 1, -16.6, 0),
    ("invert1", "e1", 1, -10.37, 0), ("resid1", "e1", 1, -4.76, 0),
    ("resid0", "o0", 1, -33.68, 0), ("keep0", "m0", 1, -32.36, 0), ("skip0", "o0", 1, -32.13, 0),
    ("stats2", "f0", 1, -30.7, 0), ("scale2", "f0", 1, -29.69, 0), ("rank", "f0", 1, -27.69, 0), ("onehot", "f0", 1, -27.25, 0),
    ("pick", "f0", 1, -23.95, 0), ("picked", "f0", 1, -26.27, 0), ("up2", "f0", 2, -21.56, 2.793), ("bias2", "f0", 2, -21.85, 2.424),
    ("square2", "f0", 1, -20.02, 0), ("inner2", "f0", 1, -14.47, 0), ("tanh2", "f0", 1, -9.8, 0), ("gelu2", "f0", 1, -14.65, 0),
    ("turnmax0", "m0", 1, -10.0, 0), ("shift0", "m0", 1, -8.47, 0),
    ("down2", "f0", 1, -6.32, 0), ("half2", "f0", 1, -4.32, 0), ("spread", "f0", 1, -6.09, 0), ("add2", "f0", 1, -2.69, 0),
)

LAG = {
    ("act", "shift1"): 0.67,
    ("dve", "add3"): 0.12,
    ("dve", "gelu2"): 0.69,
    ("dve", "invert1"): -0.25,
    ("dve", "scale3"): 0.29,
    ("dve", "shift1"): -0.17,
    ("dve", "stats3"): -0.03,
    ("pe", "exp1more"): -0.55,
    ("pe", "max1"): 0.44,
    ("pe", "values1"): 1.75,
    ("sp", "assemble0"): 0.04,
    ("sp", "keys1"): 1.16,
    ("sp", "out0last"): -0.01,
    ("sp", "store0"): -2.58,
    ("sp", "store1"): -0.37,
}

LOOKUPS = (
    (-1, -36.39), (-1, -26.96), (-1, -9.81), (-1, 12.73), (0, 5.24), (0, 17.44), (0, 20.03), (1, -16),
    (1, 8.8), (1, 9.67), (1, 41.36), (2, -17.95),
)


def lim(count):
    return min(count, NP) if isinstance(count, int) else count


def due(count):
    return not isinstance(count, int) or count > 0


def settle(eng, passed, count=None):
    if not isinstance(count, int):
        eng.sem_inc(passed, 1)


def flamingo_kernel(nc, a, out):
    with ExitStack() as ctx:
        def sb(name, shape, dt=F32):
            return ctx.enter_context(nc.sbuf_tensor(name, shape, dt))

        def ps(name):
            return ctx.enter_context(nc.psum_tensor(name, [128, 512], F32))

        def sem(name):
            return ctx.enter_context(nc.semaphore(name))

        ident = sb("ident", [128, 128])
        tril = sb("tril", [128, 128])
        iota = sb("iota", [128, KEEP])
        wq, wk, wv = sb("wq", [128, 128]), sb("wk", [128, 128]), sb("wv", [128, 128])
        bqk = sb("bqk", [128, 2])
        bv = sb("bv", [128, 128])
        wr = sb("wr", [128, T])
        br = sb("br", [128, 1])
        w1 = sb("w1", [128, 2, DF])
        b1 = sb("b1", [128, FC])
        w2 = sb("w2", [128, FC, T])
        b2 = sb("b2", [128, T])
        wg = sb("wg", [128, 2, INTER])
        wu = sb("wu", [128, 2, INTER])
        wd = sb("wd", [128, OC, T])
        lut = sb("lut", [128, LUT], U32)
        lutx = sb("lutx", [128, LUT // 2], U32)
        gts = sb("gts", [128, 5])
        tg = sb("tg", [128, 4])
        tgx = sb("tgx", [128, 2])

        mhalf = sb("mhalf", [128, NB])
        xin, xr0, x1, x2, x3 = (sb(n, [128, NB, T]) for n in ("xin", "xr0", "x1", "x2", "x3"))
        ctx0, ctx1 = sb("ctx0", [128, NB, T]), sb("ctx1", [128, NB, T])
        xn0, xnm, xnf1 = (sb(n, [128, NB, T]) for n in ("xn0", "xnm", "xnf1"))
        mrA = sb("mrA", [128, NB, T])
        mden = sb("mden", [128, L0.H * N // 128])
        mc = sb("mc", [128, NB * 2])
        stat = [sb(f"stat{i}", [128, NB, 6]) for i in range(4)]
        mv = [sb(f"mv{i}", [128, NB, 2]) for i in range(4)]
        rstd = [sb(f"rstd{i}", [128, NB]) for i in range(4)]

        qf = sb("qf", [128, N])
        kf = sb("kf", [128, N])
        vf = sb("vf", [128, N])
        qhl, khl = sb("qhl", [128, 2, N], F32R), sb("khl", [128, 2, N], F32R)
        orows = sb("orows", [128, N])
        chi, clo = orows[0:L0.H, :].bitcast(F32R), orows[32:32 + L0.H, :].bitcast(F32R)
        mt = orows[64:66, :].bitcast(F32R)
        ng = orows[96:98, :].bitcast(F32R)
        negs = sb("negs", [128, 1])
        QT = [[sb(f"QT0{s}", [128, L0.NG, N], F32R) for s in range(2)], [sb("QT1", [128, L1.NG, N], F32R)] * 2]
        KM = [sb(f"KM{i}", [128, L.H, N], F32R) for i, L in enumerate((L0, L1))]
        VW = (2 * L0.DH, 2 * L1.DH)
        V = [sb(f"V{i}", [128, 2 * NB, L.H, VW[i]]) for i, L in enumerate((L0, L1))]
        mx = [sb(f"mx{i}", [128, NB, 2, L.H]) for i, L in enumerate((L0, L1))]
        PR = 8
        P = sb("P", [128, PR, 512])
        ones = P[0:2, PR - 1, :]
        OG = sb("OG", [128, 2, 512])
        Oc, Dc = sb("Oc", [128, N]), sb("Dc", [128, N])
        Dn = sb("Dn", [128, 64])

        def scratch(name, shape):
            return nc.dram_tensor(name, shape, F32, kind="Internal").ap()

        q_parts = [scratch(f"q_parts{i}", (2, 128, N)) for i in range(2)]
        k_parts = [scratch(f"k_parts{i}", (2, 128, N)) for i in range(2)]
        shifts = [scratch(f"shifts{i}", (L.H, 2, N)) for i, L in enumerate((L0, L1))]
        outputs = [scratch(f"outputs{i}", (L.H, 32, N)) for i, L in enumerate((L0, L1))]
        recips = [scratch(f"recips{i}", (L.H, N)) for i, L in enumerate((L0, L1))]

        rs = sb("rs", [128, NB, 4])
        prod = sb("prod", [128, T])
        sbc = sb("sbc", [128, NB, 128])
        oh = sb("oh", [128, NB, KEEP])
        ohT = sb("ohT", [128, 128])
        xsT = sb("xsT", [128, 2, 128])
        z = sb("z", [128, DF])
        gz = sb("gz", [128, DF])
        y0 = sb("y0", [128, T])

        arena = sb("arena", [128, 2816])
        h1 = arena[:, 0:1536].rearrange("p (o n) -> p o n", o=OC)
        xT = arena[:, 1536:2048].rearrange("p (d n) -> p d n", d=2)
        th = arena[:, 2048:2560].rearrange("p (k n) -> p k n", k=2)
        ga1 = arena[:, 2560:2816]
        CH = 384
        lk = [arena[:, CH * j:CH * (j + 1)].bitcast(U32) for j in range(7)]

        mxp = [ps("mxp0"), ps("mxp1")]
        exq = [ps("exq0"), ps("exq1"), ps("exq2")]
        pv = ps("pv")
        pa = ps("pa")
        pf = ps("pf")

        def by_layer(name):
            return [sem(f"{name}{i}") for i in range(2)]

        weights_loaded = sem("weights_loaded")
        router_loaded = sem("router_loaded")
        mlp0_loaded = sem("mlp0_loaded")
        indices_loaded = sem("indices_loaded")
        pair_loaded = sem("pair_loaded")
        context1_loaded = sem("context1_loaded")
        target_mask_loaded = sem("target_mask_loaded")
        buffers_set = sem("buffers_set")
        ones_in_place = sem("ones_in_place")
        mhalf_set = sem("mhalf_set")
        gates_ready = sem("gates_ready")
        looked_up = sem("looked_up")
        norm_steps = [sem(f"norm_steps{i}") for i in range(4)]
        residual_kept = sem("residual_kept")
        q_projected = sem("q_projected")
        q_read = sem("q_read")
        k_projected = sem("k_projected")
        k_read = sem("k_read")
        v_projected = sem("v_projected")
        v_read = sem("v_read")
        split0_done = sem("split0_done")
        split1_done = sem("split1_done")
        mask_rows_ready = sem("mask_rows_ready")
        values0_ready = sem("values0_ready")
        context1_turned = sem("context1_turned")
        values1_ready = sem("values1_ready")
        q_stored = by_layer("q_stored")
        k_stored = by_layer("k_stored")
        q_in_place = by_layer("q_in_place")
        k_in_place = [[sem(f"k_in_place{i}{g}") for g in range(L.HPG)] for i, L in enumerate((L0, L1))]
        mask_in_place = sem("mask_in_place")
        max_scores_ready = by_layer("max_scores_ready")
        maxima_ready = by_layer("maxima_ready")
        maxima_turned = by_layer("maxima_turned")
        shift_high_ready = by_layer("shift_high_ready")
        shift_ready = by_layer("shift_ready")
        shift_stored = by_layer("shift_stored")
        shift_in_place = by_layer("shift_in_place")
        exp_scores_ready = by_layer("exp_scores_ready")
        probs_ready = by_layer("probs_ready")
        outputs_ready = by_layer("outputs_ready")
        outputs_read = by_layer("outputs_read")
        outputs_stored = [[sem(f"outputs_stored{i}{j}") for j in range(2)] for i in range(2)]
        denominators_gathered = by_layer("denominators_gathered")
        outputs_gathered = by_layer("outputs_gathered")
        inverse_ready = sem("inverse_ready")
        reciprocals_ready = by_layer("reciprocals_ready")
        reciprocals_stored = by_layer("reciprocals_stored")
        reciprocals_spread = by_layer("reciprocals_spread")
        outputs_divided = by_layer("outputs_divided")
        attention_added = by_layer("attention_added")
        router_steps = sem("router_steps")
        ties_found = sem("ties_found")
        router_turned = sem("router_turned")
        tokens_picked = sem("tokens_picked")
        tokens_read = sem("tokens_read")
        hidden_ready = sem("hidden_ready")
        hidden_read = sem("hidden_read")
        gelu_squared = sem("gelu_squared")
        gelu_inner = sem("gelu_inner")
        gelu_tanh = sem("gelu_tanh")
        gelu_ready = sem("gelu_ready")
        kept_ready = sem("kept_ready")
        kept_read = sem("kept_read")
        first_spread = sem("first_spread")
        kept_spread = sem("kept_spread")
        mlp0_added = sem("mlp0_added")
        x3_turned = sem("x3_turned")
        x3_read = sem("x3_read")
        gate_up_ready = sem("gate_up_ready")
        silu_tanh = sem("silu_tanh")
        silu_gate = sem("silu_gate")
        silu_ready = sem("silu_ready")
        down_ready = sem("down_ready")
        mlp1_added = sem("mlp1_added")
        stored = sem("stored")
        passed_sp, passed_dve, passed_pool = sem("passed_sp"), sem("passed_dve"), sem("passed_pool")

        def f32(ap):
            return ap.bitcast(F32)

        block = ctx.enter_context(nc.Block())


        def unit(L, k):
            return L.HPG * (k % 4) + k // 8, k // 4 % 2

        def max_unit(L, k):
            g, G = k // (2 * L.NG), k // 2 % L.NG
            return L.HPG * G + g, k % 2, g

        LKC = 19
        LKN = LKC * 12

        def lookup_chunk(c):
            if c < 8:
                w = (wg, wu)[c // 4]
                return w[:, :, :].rearrange("p d n -> p (d n)"), (c % 4) * 344, 344
            return wd[:, :, :].rearrange("p o n -> p (o n)"), (c - 8) * 384, 384

        def steps(engine, i, turn, **there):
            plan = [(at + LAG.get((engine, name), 0) + apart * k, name, i + PAIR[stage], k, (turn + PAIR[stage]) % 2)
                    for name, stage, parts, at, apart in STEPS if there.get(stage, True) for k in range(parts)]
            plan += [(at, "lookup", 0, k, 0) for k, (when, at) in enumerate(LOOKUPS) if isinstance(i, int) and when == i]
            for _, name, p, k, slot in sorted(plan, key=lambda s: s[0]):
                name, k = whole(name, k)
                yield name, p, k, slot

        def program(engine, eng, step):
            for i in (-1, 0, 1, 2):
                for step_of in steps(engine, i, i, m0=i >= 0, e0=i >= 0, o0=i >= 1, f0=i >= 1, m1=i >= 1,
                                     e1=i >= 2, f1=i >= 2):
                    step(*step_of)
            with eng.Fori(3, NP - 2, 2) as i:
                for turn in (1, 2):
                    for step_of in steps(engine, i + turn - 1, turn):
                        step(*step_of)
            for i in (NP - 1, NP, NP + 1):
                for step_of in steps(engine, i, i, n0=False, a0=False, m0=i < NP, e0=i < NP, o0=i <= NP, f0=i <= NP,
                                     m1=i <= NP):
                    step(*step_of)

        def layer(name):
            i = int(name[-1])
            return i, (L0, L1)[i]

        def whole(name, k):
            if name.endswith("last"):
                name = name[:-4]
                return name, {"pv0": L0.U // 4, "pv1": L1.U // 4, "out0": L0.NT, "out1": L1.NT}[name] - 1
            return (name[:-4], k + (8 if name == "max0more" else 4)) if name.endswith("more") else (name, k)

        @block.sync
        def _(sp):
            def rows(ap):
                return ap.rearrange("(a d) -> a d", a=1)

            def inputs0(p):
                if due(p):
                    sp.wait_ge(residual_kept, p)
                settle(sp, passed_sp, p)
                if due(p):
                    sp.wait_ge(v_projected, p)
                settle(sp, passed_sp, p)
                if due(p):
                    sp.wait_ge(values0_ready, p)
                settle(sp, passed_sp, p)
                if due(2 * p):
                    sp.wait_ge(mask_rows_ready, 2 * p)
                settle(sp, passed_sp, 2 * p)
                if due(6 * p):
                    sp.wait_ge(split0_done, 6 * p)
                settle(sp, passed_sp, 6 * p)
                pair = bass.ds(p * NB, NB)
                sp.dma_start(xin[:, :, :], a["x"][pair].rearrange("b c t -> c b t")).then_inc(pair_loaded, 16)
                sp.dma_start(ctx0[:, :, :], a["ctx_2048"][pair].rearrange("b c t -> c b t")).then_inc(pair_loaded, 16)
                sp.dma_start(mrA[:, :, :].rearrange("p b t -> p (b t)"),
                             a["mrow"][bass.ds(p, 1), :].to_broadcast([128, N])).then_inc(pair_loaded, 16)
                sp.dma_start(mc[:, :], a["mcol"][bass.ds(p, 1)].rearrange("a p k -> (a p) k")).then_inc(pair_loaded, 16)

            def context1(p):
                if due(4 * p):
                    sp.wait_ge(split1_done, 4 * p)
                settle(sp, passed_sp, 4 * p)
                if due(p):
                    sp.wait_ge(context1_turned, p)
                settle(sp, passed_sp, p)
                sp.dma_start(ctx1[:, :, :], a["ctx_2048"][bass.ds(p * NB, NB)].rearrange("b c t -> c b t")).then_inc(context1_loaded, 16)

            def target_mask(p):
                if due(p):
                    sp.wait_ge(reciprocals_ready[0], p)
                settle(sp, passed_sp, p)
                sp.dma_start(mden[:, :], a["mrow"][bass.ds(p, 1), :].rearrange("a (j n) -> a j n", j=8)
                             .to_broadcast([L0.H, 8, N // 8])).then_inc(target_mask_loaded, 16)

            for dst, src in ((ident, a["ident"]), (wq, a["wqT"]), (wk, a["wkT"]), (wv, a["wvT"]), (bqk, a["bqk"])):
                sp.dma_start(dst[:, :], src).then_inc(weights_loaded, 16)
            sp.dma_start(bv[:, :], rows(a["L0_xattn_bv"]).to_broadcast([128, 128])).then_inc(weights_loaded, 16)
            sp.dma_start(gts[:, :], a["gts"].to_broadcast([128, 5])).then_inc(weights_loaded, 16)
            sp.dma_start(negs[96:98, :], a["negs"]).then_inc(weights_loaded, 16)
            sp.dma_start(tril[:, :], a["tril"]).then_inc(router_loaded, 16)
            sp.dma_start(iota[:, :], a["iota"].to_broadcast([128, KEEP])).then_inc(router_loaded, 16)
            sp.dma_start(wr[:, :], rows(a["L0_ffn_w_r"]).to_broadcast([128, T])).then_inc(router_loaded, 16)
            sp.dma_start(br[:, :], a["br"].to_broadcast([128, 1])).then_inc(router_loaded, 16)
            sp.dma_start(lut[:, :], rows(a["L1_ffn_lut"]).to_broadcast([128, LUT]).bitcast(U32)).then_inc(router_loaded, 16)
            sp.dma_start(wg[:, :, :].bitcast(I32), a["gate_i"]).then_inc(indices_loaded, 16)
            sp.dma_start(wu[:, :, :].bitcast(I32), a["up_i"]).then_inc(indices_loaded, 16)
            sp.dma_start(wd[:, :, :].bitcast(I32), a["down_i"]).then_inc(indices_loaded, 16)
            sp.wait_ge(buffers_set, 6)
            for L, km in ((L0, KM[0]), (L1, KM[1])):
                for g in range(L.HPG):
                    r = L.SHIFT + 2 * g
                    sp.dma_start(f32(km[r:r + 2, g::L.HPG, :]),
                                 ones[:, :].unsqueeze(1).to_broadcast([2, L.NG, N])).then_inc(ones_in_place, 16)
            sp.dma_start(w1[:, :, :], a["L0_ffn_w1"].rearrange("(k p) n -> p k n", p=128)).then_inc(mlp0_loaded, 16)
            sp.dma_start(b1[:, :], a["b1c"]).then_inc(mlp0_loaded, 16)
            sp.dma_start(w2[:, :, :], a["L0_ffn_w2"].rearrange("(k p) n -> p k n", p=128)).then_inc(mlp0_loaded, 16)
            sp.dma_start(b2[:, :], rows(a["L0_ffn_b2"]).to_broadcast([128, T])).then_inc(mlp0_loaded, 16)

            def step(name, p, k, slot):
                if name in ("store0", "store1"):
                    i, L = layer(name)
                    for half, (src, dst, written, read) in enumerate(((qhl, q_parts, q_stored, q_in_place), (khl, k_parts, k_stored, k_in_place))):
                        done = (6, 4)[i] * p + ((3, 6), (2, 4))[i][half]
                        sp.wait_ge((split0_done, split1_done)[i], done)
                        settle(sp, passed_sp, done)
                        if half == 0:
                            if due(p):
                                sp.wait_ge(q_in_place[i], 48 * p)
                            settle(sp, passed_sp, p)
                        else:
                            for g in range(L.HPG):
                                if due(p):
                                    sp.wait_ge(k_in_place[i][g], (64, 48)[i] * p)
                                settle(sp, passed_sp, p)
                        sp.dma_start(dst[i].rearrange("j p n -> p j n"), f32(src[:, :, :])).then_inc(written[i], 16)
                elif name in ("assemble0", "assemble1"):
                    i, L = layer(name)
                    sp.wait_ge(q_stored[i], 16 * (p + 1))
                    settle(sp, passed_sp, p)
                    if due(p - 1 if i == 0 else p):
                        sp.wait_ge(exp_scores_ready[i], L.U * (p - 1 if i == 0 else p))
                    settle(sp, passed_sp, p)
                    q = q_parts[i].rearrange("j (G p) n -> j p G n", G=L.NG)
                    for j, part in enumerate((0, 0, 1)):
                        sp.dma_start(f32(QT[i][slot][32 * j:32 * j + 32, :, :]), q[part]).then_inc(q_in_place[i], 16)
                    if i == 0:
                        sp.wait_ge(mask_rows_ready, 2 * (p + 1))
                        settle(sp, passed_sp, p)
                        sp.dma_start(f32(QT[0][slot][96:98, :, :]),
                                     f32(mt[:, :]).unsqueeze(1).to_broadcast([2, L.NG, N])).then_inc(mask_in_place, 16)
                elif name in ("keys0", "keys1"):
                    i, L = layer(name)
                    if k == 0:
                        sp.wait_ge(k_stored[i], 16 * (p + 1))
                        settle(sp, passed_sp, p)
                        if i == 0:
                            sp.wait_ge(mask_rows_ready, 2 * (p + 1))
                            settle(sp, passed_sp, p)
                    if due(p):
                        sp.wait_ge(exp_scores_ready[i], L.U * p - L.U + 8 * k + 8)
                    settle(sp, passed_sp, p)
                    keys = k_parts[i].rearrange("j (G g d) n -> j g d G n", G=L.NG, g=L.HPG)
                    for j, part in enumerate((0, 1, 0)):
                        r = 32 * j + L.DH * k
                        sp.dma_start(f32(KM[i][r:r + L.DH, k::L.HPG, :]), keys[part, k]).then_inc(k_in_place[i][k], 16)
                    if i == 0:
                        sp.dma_start(f32(KM[0][96:98, k::L.HPG, :]),
                                     f32(ng[:, :]).unsqueeze(1).to_broadcast([2, L.NG, N])).then_inc(k_in_place[0][k], 16)
                elif name in ("shift0", "shift1"):
                    i, L = layer(name)
                    sp.wait_ge(shift_ready[i], p + 1)
                    settle(sp, passed_sp, p)
                    if due(p):
                        sp.wait_ge(shift_in_place[i], 16 * p)
                    settle(sp, passed_sp, p)
                    for j, src in enumerate((chi, clo)):
                        sp.dma_start(shifts[i][:, j, :], f32(src[0:L.H, :])).then_inc(shift_stored[i], 16)
                    sp.wait_ge(shift_stored[i], 32 * (p + 1))
                    settle(sp, passed_sp, p)
                    sp.dma_start(f32(QT[i][slot][L.SHIFT:L.KE, :, :]),
                                 shifts[i].rearrange("(G g) j n -> (g j) G n", G=L.NG)).then_inc(shift_in_place[i], 16)
                elif name in ("out0", "out1"):
                    i, L = layer(name)
                    sp.wait_ge(outputs_read[i], L.NT * p + k + 1)
                    settle(sp, passed_sp, p)
                    if k == 0:
                        if due(p):
                            sp.wait_ge(outputs_gathered[i], 16 * p)
                        settle(sp, passed_sp, p)
                        if due(p):
                            sp.wait_ge(denominators_gathered[i], 16 * p)
                        settle(sp, passed_sp, p)
                    sp.dma_start(outputs[i][k::L.HPG],
                                 OG[:, k % 2, :]).then_inc(outputs_stored[i][k % 2], 16)
                elif name in ("gather0", "gather1"):
                    i, L = layer(name)
                    for slot in range(2):
                        sp.wait_ge(outputs_stored[i][slot], 8 * L.NT * (p + 1))
                        settle(sp, passed_sp, p)
                    if i == 0:
                        if due(p - 1):
                            sp.wait_ge(attention_added[1], p - 1)
                        settle(sp, passed_sp, p - 1)
                        if due(p):
                            sp.wait_ge(attention_added[0], p)
                        settle(sp, passed_sp, p)
                    else:
                        sp.wait_ge(attention_added[0], lim(p + 2))
                        settle(sp, passed_sp, p)
                    w = L.H * N // 128
                    sp.dma_start(Dn[:, 0:w], outputs[i][:, L.DH, :].rearrange("h (j n) -> h j n", n=w)).then_inc(denominators_gathered[i], 16)
                    sp.dma_start(Oc[:, :], outputs[i][:, 0:L.DH, :]).then_inc(outputs_gathered[i], 16)
                elif name in ("invert0", "invert1"):
                    i, L = layer(name)
                    w = L.H * N // 128
                    sp.wait_ge(reciprocals_ready[i], p + 1)
                    settle(sp, passed_sp, p)
                    sp.dma_start(recips[i].rearrange("h (j n) -> h j n", n=w), Dn[:, 0:w]).then_inc(reciprocals_stored[i], 16)
                    sp.wait_ge(reciprocals_stored[i], 16 * (p + 1))
                    settle(sp, passed_sp, p)
                    sp.dma_start(Dc[:, :], recips[i].unsqueeze(1).to_broadcast([L.H, L.DH, N])).then_inc(reciprocals_spread[i], 16)
                elif name == "load":
                    inputs0(p)
                elif name == "keep0":
                    target_mask(p)
                elif name == "skip0":
                    context1(p)
                elif name == "add3":
                    sp.wait_ge(mlp1_added, p + 1)
                    settle(sp, passed_sp, p + 1)
                    sp.dma_start(out[bass.ds(p * NB, NB)].rearrange("b c t -> c b t"), xnf1[:, :, :]).then_inc(stored, 16)

            program("sp", sp, step)
            sp.wait_ge(stored, 16 * NP)

        @block.tensor
        def _(pe):
            def mm(o, l, r, start=True, stop=True):
                return nc.tensor.matmul(o, l, r, start=start, stop=stop, skip_group_check=True)

            def step(name, p, k, slot):
                if name == "query0":
                    pe.wait_ge(weights_loaded, 16 * 8)
                    pe.wait_ge(norm_steps[0], 8 * (p + 1))
                    if due(p - 1):
                        pe.wait_ge(shift_ready[0], p - 1)
                    if due(p - 2):
                        pe.wait_ge(shift_ready[1], p - 2)
                    mm(pa[:, :], wq[:, :], xn0[:, :, :].rearrange("p b t -> p (b t)")).then_inc(q_projected, 1)
                elif name == "key0":
                    pe.wait_ge(pair_loaded, 64 * (p + 1))
                    pe.wait_ge(q_read, p + 1)
                    mm(pa[:, :], wk[:, :], ctx0[:, :, :].rearrange("p b t -> p (b t)")).then_inc(k_projected, 1)
                elif name == "value0":
                    pe.wait_ge(k_read, p + 1)
                    for b in range(NB):
                        for s in range(2):
                            j = 2 * b + s
                            last = mm(pa[:, 128 * j:128 * j + 128], ctx0[:, b, 128 * s:128 * s + 128], wv[:, :])
                    last.then_inc(v_projected, 1)
                elif name == "values1":
                    pe.wait_ge(context1_loaded, 16 * (p + 1))
                    pe.wait_ge(shift_ready[0], lim(p + 2))
                    for b in range(NB):
                        for s in range(2):
                            j = 2 * b + s
                            last = nc.tensor.transpose(pa[:, 128 * j:128 * j + 128],
                                                       ctx1[:, b, 128 * s:128 * s + 128], ident[:, :])
                    last.then_inc(context1_turned, 1)
                elif name in ("max0", "max1"):
                    i, L = layer(name)
                    h, b, g = max_unit(L, k)
                    if k % (2 * L.NG) == 0:
                        pe.wait_ge(k_in_place[i][g], (64, 48)[i] * (p + 1))
                    if k == 0:
                        pe.wait_ge(q_in_place[i], 48 * (p + 1))
                        if i == 0:
                            pe.wait_ge(mask_in_place, 16 * (p + 1))
                        pe.wait_ge(ones_in_place, 16 * (L0.HPG + L1.HPG))
                        if i == 0:
                            if due(L1.U * (p - 1)):
                                pe.wait_ge(maxima_ready[1], L1.U * (p - 1))
                            if due(L0.U * p):
                                pe.wait_ge(maxima_ready[0], L0.U * p)
                        else:
                            pe.wait_ge(maxima_ready[0], L0.U * lim(p + 2))
                    elif k >= 2:
                        if due(L.U * p + k - 1):
                            pe.wait_ge(maxima_ready[i], L.U * p + k - 1)
                    for s in range(2):
                        q0 = b * T + 128 * s
                        last = mm(mxp[k % 2][:, T * s:T * s + T], QT[i][slot][0:L.SHIFT, h // L.HPG, q0:q0 + 128],
                                  KM[i][0:L.SHIFT, h, b * T:b * T + T])
                    last.then_inc(max_scores_ready[i], 1)
                elif name in ("turnmax0", "turnmax1"):
                    i, L = layer(name)
                    pe.wait_ge(maxima_ready[i], L.U * (p + 1))
                    if i == 0:
                        if due(p - 1):
                            pe.wait_ge(shift_ready[1], p - 1)
                        pe.wait_ge(v_read, lim(p + 2))
                    else:
                        pe.wait_ge(values1_ready, p + 1)
                    for b in range(NB):
                        for s in range(2):
                            j = 2 * b + s
                            last = mm(pa[0:L.H, 128 * j:128 * j + 128], mx[i][:, b, s, :], ident[:, :])
                    last.then_inc(maxima_turned[i], 1)
                elif name in ("exp0", "exp1"):
                    i, L = layer(name)
                    if k == 0:
                        pe.wait_ge(shift_in_place[i], 16 * (p + 1))
                        if i == 0:
                            if due(L1.U * (p - 1)):
                                pe.wait_ge(probs_ready[1], L1.U * (p - 1))
                            if due(L0.U * p):
                                pe.wait_ge(probs_ready[0], L0.U * p)
                        else:
                            pe.wait_ge(probs_ready[0], L0.U * lim(p + 2))
                    if k >= 3:
                        if due(L.U * p + k - 2):
                            pe.wait_ge(probs_ready[i], L.U * p + k - 2)
                    h, b = unit(L, k)
                    for s in range(2):
                        k0 = b * T + 128 * s
                        last = mm(exq[(k + 2 * i) % 3][:, T * s:T * s + T], KM[i][0:L.KE, h, k0:k0 + 128],
                                  QT[i][slot][0:L.KE, h // L.HPG, b * T:b * T + T])
                    last.then_inc(exp_scores_ready[i], 1)
                elif name in ("pv0", "pv1"):
                    i, L = layer(name)
                    pe.wait_ge(probs_ready[i], L.U * p + 4 * k + 4)
                    if k == 0:
                        pe.wait_ge((values0_ready, values1_ready)[i], p + 1)
                        if i == 0:
                            if due(L1.NT * (p - 1)):
                                pe.wait_ge(outputs_read[1], L1.NT * (p - 1))
                            if due(L0.NT * p):
                                pe.wait_ge(outputs_read[0], L0.NT * p)
                        else:
                            pe.wait_ge(outputs_read[0], L0.NT * lim(p + 2))
                    elif k % 2 == 0:
                        if due(L.NT * p + k // 2):
                            pe.wait_ge(outputs_read[i], L.NT * p + k // 2)
                    b = k % 2
                    for s in range(2):
                        for g in range(4):
                            h = L.HPG * g + k // 2
                            last = mm(pv[32 * g:32 * g + VW[i], b * T:b * T + T], V[i][:, 2 * b + s, h, :],
                                      P[:, (4 * k + g) % PR, T * s:T * s + T], start=s == 0, stop=s == 1)
                    last.then_inc(outputs_ready[i], 1)
                elif name == "rank":
                    pe.wait_ge(router_steps, 12 * p + 6)
                    if due(p - 1):
                        pe.wait_ge(mlp1_added, p - 1)
                    if due(p):
                        pe.wait_ge(mlp0_added, p)
                    for b in range(NB):
                        last = nc.tensor.transpose(pf[:, 128 * b:128 * b + 128], sbc[:, b, :], ident[:, :])
                    last.then_inc(router_turned, 1)
                elif name == "pick":
                    if due(12 * p + 12):
                        pe.wait_ge(router_steps, 12 * p + 12)
                    for d in range(2):
                        for b in range(NB):
                            o = 128 * d + KEEP * b
                            mm(pf[:, o:o + KEEP], xnm[:, b, 128 * d:128 * d + 128], oh[:, b, :])
                    nc.tensor.transpose(pf[:, 256:384], oh[:, :, :].rearrange("p b k -> p (b k)"), ident[:, :]).then_inc(tokens_picked, 1)
                elif name == "up2":
                    if k == 0:
                        pe.wait_ge(mlp0_loaded, 16 * 4)
                        pe.wait_ge(tokens_read, 2 * (p + 1))
                    else:
                        pe.wait_ge(hidden_read, 2 * p + 1)
                    for f in range(4):
                        for d in range(2):
                            c0 = 128 * (4 * k + f)
                            last = mm(pf[:, 128 * f:128 * f + 128], w1[:, d, c0:c0 + 128], xsT[:, d, :],
                                      start=d == 0, stop=d == 1)
                    last.then_inc(hidden_ready, 1)
                elif name == "down2":
                    pe.wait_ge(gelu_ready, p + 1)
                    for f in range(FC):
                        last = mm(pf[:, 0:T], z[:, 128 * f:128 * f + 128], w2[:, f, :], start=f == 0, stop=f == FC - 1)
                    last.then_inc(kept_ready, 1)
                elif name == "spread":
                    pe.wait_ge(kept_read, p + 1)
                    mm(pf[:, 0:T], ohT[0:KEEP, :], y0[0:KEEP, :]).then_inc(first_spread, 1)
                    pe.wait_ge(first_spread, p + 1)
                    mm(pf[:, T:2 * T], ohT[KEEP:2 * KEEP, :], y0[KEEP:2 * KEEP, :]).then_inc(kept_spread, 1)
                elif name == "turn3":
                    pe.wait_ge(norm_steps[3], 8 * (p + 1))
                    pe.wait_ge(mlp0_added, lim(p + 2))
                    for d in range(2):
                        for b in range(NB):
                            o = T * d + 128 * b
                            last = nc.tensor.transpose(pf[:, o:o + 128], xnf1[:, b, 128 * d:128 * d + 128], ident[:, :])
                    last.then_inc(x3_turned, 1)
                elif name == "up3":
                    if k == 0:
                        pe.wait_ge(x3_read, p + 1)
                        pe.wait_ge(looked_up, LKN)
                    else:
                        if due(OC * p + k):
                            pe.wait_ge(silu_ready, OC * p + k)
                    for w, o in ((wg, 0), (wu, T)):
                        for d in range(2):
                            last = mm(pf[0:OM[k], o:o + T], w[:, d, 128 * k:128 * k + OM[k]], xT[:, d, :],
                                      start=d == 0, stop=d == 1)
                    last.then_inc(gate_up_ready, 1)
                elif name == "down3":
                    pe.wait_ge(silu_ready, OC * (p + 1))
                    for b in range(NB):
                        for o in range(OC):
                            last = mm(pf[:, T * b:T * b + T], h1[0:OM[o], o, 128 * b:128 * b + 128],
                                      wd[0:OM[o], o, :], start=o == 0, stop=o == OC - 1)
                    last.then_inc(down_ready, 1)

            program("pe", pe, step)

        @block.scalar
        def _(act):
            act.wait_ge(weights_loaded, 16 * 8)
            nc.scalar.activation(tg[:, :], gts[:, 0:4], ACT.Tanh).then_inc(gates_ready, 1)

            def step(name, p, k, slot):
                if name in ("query0b", "key0b"):
                    dst, prod_, done, j = ((qf, q_projected, q_read, 0), (kf, k_projected, k_read, 1))[name == "key0b"]
                    act.wait_ge(prod_, p + 1)
                    if due(6 * p):
                        act.wait_ge(split0_done, 6 * p)
                    nc.scalar.activation(dst[:, :], pa[:, :], ACT.Identity, bias=bqk[:, j:j + 1]).then_inc(done, 1)
                elif name == "values1b":
                    act.wait_ge(context1_turned, p + 1)
                    if due(L1.U // 4 * p):
                        act.wait_ge(outputs_ready[1], L1.U // 4 * p)
                    act.wait_ge(buffers_set, 6)
                    nc.scalar.copy(V[1][:, :, :, 0:L1.DH],
                                   pa[:, :].rearrange("p (j h d) -> p j h d", j=4, h=L1.H)).then_inc(values1_ready, 1)
                elif name in ("shift0", "shift1"):
                    i, L = layer(name)
                    act.wait_ge(maxima_turned[i], p + 1)
                    if i == 0:
                        if due(p - 1):
                            act.wait_ge(shift_stored[1], 32 * (p - 1))
                        if due(p):
                            act.wait_ge(shift_stored[0], 32 * p)
                    else:
                        act.wait_ge(shift_stored[0], 32 * lim(p + 2))
                    nc.scalar.activation(chi[0:L.H, :], pa[0:L.H, :], ACT.Copy, scale=-1.0).then_inc(shift_high_ready[i], 1)
                elif name in ("exp0", "exp1"):
                    i, L = layer(name)
                    act.wait_ge(exp_scores_ready[i], L.U * p + k + 1)
                    if k % 4 == 0:
                        if k >= PR:
                            act.wait_ge(outputs_ready[i], L.U // 4 * p + (k - PR) // 4 + 1)
                        elif i == 0:
                            if due(L1.U // 4 * (p - 1)):
                                act.wait_ge(outputs_ready[1], L1.U // 4 * (p - 1))
                            if due(L0.U // 4 * p):
                                act.wait_ge(outputs_ready[0], L0.U // 4 * p)
                        else:
                            act.wait_ge(outputs_ready[0], L0.U // 4 * lim(p + 2))
                    nc.scalar.activation(P[:, k % PR, :], exq[(k + 2 * i) % 3][:, :], ACT.Exp,
                                         scale=L.scale).then_inc(probs_ready[i], 1)
                elif name in ("out0", "out1"):
                    i, L = layer(name)
                    act.wait_ge(outputs_ready[i], L.U // 4 * p + 2 * k + 2)
                    if k >= 2:
                        if due(128 * (2 * p + 1)):
                            act.wait_ge(outputs_stored[i][k % 2], 16 * (2 * p + 1))
                    elif i == 0:
                        if due(p - 1):
                            act.wait_ge(outputs_stored[1][k % 2], 16 * (p - 1))
                        if due(p):
                            act.wait_ge(outputs_stored[0][k % 2], 32 * p)
                    else:
                        if due(128 * 2 * lim(p + 2)):
                            act.wait_ge(outputs_stored[0][k % 2], 32 * lim(p + 2))
                    nc.scalar.copy(OG[:, k % 2, :], pv[:, :]).then_inc(outputs_read[i], 1)
                elif name == "picked":
                    act.wait_ge(tokens_picked, p + 1)
                    if due(2 * p):
                        act.wait_ge(hidden_ready, 2 * p)
                    if due(p):
                        act.wait_ge(kept_spread, p)
                    nc.scalar.copy(xsT[:, :, :].rearrange("p d k -> p (d k)"), pf[:, 0:256]).then_inc(tokens_read, 1)
                    nc.scalar.copy(ohT[:, :], pf[:, 256:384]).then_inc(tokens_read, 1)
                elif name == "square2":
                    act.wait_ge(hidden_read, 2 * (p + 1))
                    nc.scalar.activation(gz[:, :], z[:, :], ACT.Square).then_inc(gelu_squared, 1)
                elif name == "tanh2":
                    act.wait_ge(gelu_inner, 2 * (p + 1))
                    nc.scalar.activation(gz[:, :], gz[:, :], ACT.Tanh, scale=GELU_C).then_inc(gelu_tanh, 1)
                elif name == "turned3":
                    act.wait_ge(x3_turned, p + 1)
                    if due(OC * p):
                        act.wait_ge(gate_up_ready, OC * p)
                    act.wait_ge(looked_up, LKN)
                    nc.scalar.copy(xT[:, :, :].rearrange("p d n -> p (d n)"), pf[:, :]).then_inc(x3_read, 1)
                elif name == "tanh3":
                    act.wait_ge(gate_up_ready, OC * p + k + 1)
                    if due(OC * p + max(k - 1, 0)):
                        act.wait_ge(silu_gate, OC * p + max(k - 1, 0))
                    nc.scalar.activation(th[0:OM[k], k % 2, :], pf[0:OM[k], 0:T], ACT.Tanh, scale=0.5).then_inc(silu_tanh, 1)

            program("act", act, step)

        @block.vector
        def _(dve):
            def stats(i, x, p):
                n0 = 8 * p
                if due(n0):
                    dve.wait_ge(norm_steps[i], n0)
                for b in range(NB):
                    nc.vector.bn_stats(stat[i][:, b, :], x[:, b, :]).then_inc(norm_steps[i], 1)
                dve.wait_ge(norm_steps[i], n0 + 2)
                settle(dve, passed_dve)
                for b in range(NB):
                    nc.vector.bn_aggr(mv[i][:, b, :], stat[i][:, b, :]).then_inc(norm_steps[i], 1)
                dve.wait_ge(norm_steps[i], n0 + 4)
                nc.vector.tensor_scalar(rstd[i][:, :], mv[i][:, :, 1], EPS, None, ALU.add).then_inc(norm_steps[i], 1)

            def scale(i, x, xn, p):
                dve.wait_ge(norm_steps[i], 8 * p + 6)
                for b in range(NB):
                    nc.vector.tensor_scalar(xn[:, b, :], x[:, b, :], mv[i][:, b, 0:1], rstd[i][:, b:b + 1],
                                            ALU.subtract, ALU.mult).then_inc(norm_steps[i], 1)

            def lookup(c):
                w, c0, n = lookup_chunk(c)
                idx = w[:, c0:c0 + n].bitcast(U32)
                at = [LKC * c]

                def do(ins):
                    ins.then_inc(looked_up, 1)
                    at[0] += 1
                    dve.wait_ge(looked_up, at[0])

                m0, m1, m2, m3, t1, t2, t3 = (x[:, 0:n] for x in lk)
                do(nc.vector.tensor_scalar(m0.bitcast(I32), idx.bitcast(I32), 31, 31, ALU.logical_shift_left, ALU.arith_shift_right))
                for m, bit in ((m1, 2), (m2, 4), (m3, 8)):
                    do(nc.vector.tensor_scalar(m, idx, bit, None, ALU.bitwise_and))

                def leaf(dst, j):
                    do(nc.vector.tensor_scalar(dst, m0, lutx[:, j:j + 1], lut[:, 2 * j:2 * j + 1],
                                               ALU.bitwise_and, ALU.bitwise_xor))

                def four(dst, tmp, j):
                    leaf(dst, 2 * j)
                    leaf(tmp, 2 * j + 1)
                    do(nc.vector.copy_predicated(dst, m1, tmp))

                four(idx, t1, 0)
                four(t2, t1, 1)
                do(nc.vector.copy_predicated(idx, m2, t2))
                four(t2, t1, 2)
                four(t3, t1, 3)
                do(nc.vector.copy_predicated(t2, m2, t3))
                do(nc.vector.copy_predicated(idx, m3, t2))
                assert at[0] == LKC * (c + 1)

            nc.vector.memset(f32(KM[0][:, :, :]), 0.0).then_inc(buffers_set, 1)
            nc.vector.memset(ones[:, :], 1.0).then_inc(buffers_set, 1)
            nc.vector.memset(pv[:, :], 0.0).then_inc(buffers_set, 1)
            nc.vector.memset(f32(KM[1][:, :, :]), 0.0).then_inc(buffers_set, 1)
            dve.wait_ge(gates_ready, 1)
            nc.vector.tensor_tensor(tgx[:, 0:1], tg[:, 2:3], gts[:, 4:5], ALU.mult).then_inc(gates_ready, 1)
            nc.vector.tensor_scalar(tgx[:, 1:2], tg[:, 3:4], 0.5, None, ALU.mult).then_inc(gates_ready, 1)
            dve.wait_ge(router_loaded, 16 * 5)
            lv = lut[:, :].rearrange("p (j two) -> p j two", two=2)
            nc.vector.tensor_tensor(lutx[:, :], lv[:, :, 0], lv[:, :, 1], ALU.bitwise_xor).then_inc(gates_ready, 1)
            dve.wait_ge(gates_ready, 4)
            dve.wait_ge(indices_loaded, 16 * 3)

            def flat(t):
                return t[:, :, :].rearrange("p b t -> p (b t)")

            def step(name, p, k, slot):
                if name == "stats0":
                    dve.wait_ge(pair_loaded, 64 * (p + 1))
                    stats(0, xin, p)
                elif name == "scale0":
                    if due(p):
                        dve.wait_ge(q_projected, p)
                    scale(0, xin, xn0, p)
                elif name == "stats1":
                    dve.wait_ge(mlp0_added, p + 1)
                    stats(2, x2, p)
                elif name == "scale1":
                    dve.wait_ge(tokens_picked, p + 1)
                    if due(p):
                        dve.wait_ge(split1_done, 4 * p)
                    scale(2, x2, xnm, p)
                elif name == "stats3":
                    dve.wait_ge(attention_added[1], p + 1)
                    stats(3, x3, p)
                elif name == "scale3":
                    if due(p):
                        dve.wait_ge(stored, 16 * p)
                    scale(3, x3, xnf1, p)
                elif name == "lookup":
                    lookup(k)
                elif name == "masks0":
                    if due(p):
                        dve.wait_ge(mask_in_place, 16 * p)
                        for g in range(L0.HPG):
                            dve.wait_ge(k_in_place[0][g], 64 * p)
                    m = mrA[:, :, :].rearrange("p b t -> p (b t)")
                    nc.vector.tensor_scalar(mt[:, :], m[64:66, :], 1.0, None, ALU.mult).then_inc(mask_rows_ready, 1)
                    nc.vector.tensor_scalar(ng[:, :], m[96:98, :], -1.0, negs[96:98, 0:1], ALU.add, ALU.mult).then_inc(mask_rows_ready, 1)
                elif name == "value0b":
                    dve.wait_ge(v_projected, p + 1)
                    if due(p):
                        dve.wait_ge(values0_ready, p)
                    nc.vector.tensor_tensor(vf[:, :].rearrange("p (j n) -> p j n", j=4),
                                            pa[:, :].rearrange("p (j n) -> p j n", j=4),
                                            bv[:, :].unsqueeze(1).to_broadcast([128, 4, 128]), ALU.add).then_inc(v_read, 1)
                elif name in ("max0", "max1"):
                    i, L = layer(name)
                    dve.wait_ge(max_scores_ready[i], L.U * p + k + 1)
                    if k == 0 and due(p):
                        dve.wait_ge(maxima_turned[i], p)
                    h, b, _ = max_unit(L, k)
                    nc.vector.tensor_reduce(mx[i][:, b, :, h], mxp[k % 2][:, :].rearrange("p (s t) -> p s t", s=2),
                                            AX.X, ALU.max).then_inc(maxima_ready[i], 1)
                elif name in ("shift0", "shift1"):
                    i, L = layer(name)
                    dve.wait_ge(shift_high_ready[i], p + 1)
                    nc.vector.scalar_tensor_tensor(out=clo[0:L.H, :], in0=pa[0:L.H, :], scalar=-1.0,
                                                   in1=f32(chi[0:L.H, :]), op0=ALU.mult,
                                                   op1=ALU.subtract).then_inc(shift_ready[i], 1)
                elif name in ("resid0", "resid1"):
                    i, L = layer(name)
                    dve.wait_ge(outputs_gathered[i], 16 * (p + 1))
                    dve.wait_ge(reciprocals_spread[i], 16 * (p + 1))
                    nc.vector.tensor_tensor(Oc[:, :], Oc[:, :], Dc[:, :], ALU.mult).then_inc(outputs_divided[i], 1)
                    if i == 1:
                        dve.wait_ge(outputs_divided[1], p + 1)
                        if due(p):
                            dve.wait_ge(mlp1_added, p)
                        nc.vector.scalar_tensor_tensor(out=flat(x3), in0=Oc[:, :], scalar=tgx[:, 0:1], in1=flat(x2),
                                                       op0=ALU.mult, op1=ALU.add).then_inc(attention_added[1], 1)
                elif name == "skip0":
                    dve.wait_ge(outputs_divided[0], p + 1)
                    dve.wait_ge(residual_kept, p + 1)
                    if due(p):
                        dve.wait_ge(mlp0_added, p)
                    dve.wait_ge(gates_ready, 4)
                    nc.vector.scalar_tensor_tensor(out=flat(x1), in0=Oc[:, :], scalar=tg[:, 0:1], in1=flat(xr0),
                                                   op0=ALU.mult, op1=ALU.add).then_inc(attention_added[0], 1)
                elif name in ("invert0", "invert1"):
                    i, L = layer(name)
                    dve.wait_ge(denominators_gathered[i], 16 * (p + 1))
                    w = L.H * N // 128
                    nc.vector.reciprocal(Dn[:, 0:w], Dn[:, 0:w]).then_inc((inverse_ready, reciprocals_ready[1])[i], 1)
                    if i == 0:
                        dve.wait_ge(inverse_ready, p + 1)
                        dve.wait_ge(target_mask_loaded, 16 * (p + 1))
                        nc.vector.tensor_tensor(Dn[:, :], Dn[:, :], mden[:, :], ALU.mult).then_inc(reciprocals_ready[0], 1)
                elif name == "stats2":
                    dve.wait_ge(attention_added[0], p + 1)
                    stats(1, x1, p)
                elif name == "scale2":
                    if due(p):
                        dve.wait_ge(tokens_picked, p)
                        dve.wait_ge(split1_done, 4 * p)
                    scale(1, x1, xnm, p)
                    dve.wait_ge(norm_steps[1], 8 * (p + 1))
                    if due(p):
                        dve.wait_ge(router_turned, p)
                    if due(12 * p):
                        dve.wait_ge(router_steps, 12 * p)
                    for b in range(NB):
                        if due(12 * p + b):
                            dve.wait_ge(router_steps, 12 * p + b)
                        settle(dve, passed_dve)
                        nc.vector.tensor_tensor_reduce(prod[:, :], xnm[:, b, :], wr[:, :], 1.0, 0.0, ALU.mult,
                                                       ALU.add, rs[:, b, 0:1]).then_inc(router_steps, 1)
                    dve.wait_ge(router_steps, 12 * p + 2)
                    for b in range(NB):
                        nc.vector.tensor_scalar(rs[:, b, 1:2], rs[:, b, 0:1], br[:, 0:1], None, ALU.add).then_inc(router_steps, 1)
                    dve.wait_ge(router_steps, 12 * p + 4)
                    for b in range(NB):
                        nc.vector.tensor_scalar(sbc[:, b, :], tril[:, :], 0.0, rs[:, b, 1:2], ALU.mult,
                                                ALU.add).then_inc(router_steps, 1)
                elif name == "onehot":
                    dve.wait_ge(router_turned, p + 1)
                    if due(p):
                        dve.wait_ge(tokens_picked, p)
                    for b in range(NB):
                        row = pf[:, 128 * b:128 * b + 128]
                        nc.vector.tensor_scalar(prod[:, 0:128], row, rs[:, b, 1:2], None, ALU.is_gt).then_inc(router_steps, 1)
                        nc.vector.scalar_tensor_tensor(out=prod[:, 128:256], in0=row, scalar=rs[:, b, 1:2],
                                                       in1=tril[:, :], op0=ALU.is_equal, op1=ALU.mult).then_inc(ties_found, 1)
                        dve.wait_ge(ties_found, 2 * p + b + 1)
                        dve.wait_ge(router_steps, 12 * p + 7 + 3 * b)
                        settle(dve, passed_dve)
                        nc.vector.tensor_tensor_reduce(prod[:, 0:128], prod[:, 0:128], prod[:, 128:256], 1.0, 0.0,
                                                       ALU.add, ALU.add, rs[:, b, 2:3]).then_inc(router_steps, 1)
                        dve.wait_ge(router_steps, 12 * p + 8 + 3 * b)
                        nc.vector.tensor_scalar(oh[:, b, :], iota[:, :], rs[:, b, 2:3], None, ALU.is_equal).then_inc(router_steps, 1)
                elif name == "bias2":
                    dve.wait_ge(hidden_ready, 2 * p + k + 1)
                    if due(p):
                        dve.wait_ge(kept_ready, p)
                    nc.vector.tensor_tensor(z[:, 512 * k:512 * k + 512].rearrange("p (f n) -> p f n", f=4),
                                            pf[:, :].rearrange("p (f n) -> p f n", f=4),
                                            b1[:, 4 * k:4 * k + 4].unsqueeze(2).to_broadcast([128, 4, 128]),
                                            ALU.add).then_inc(hidden_read, 1)
                elif name == "gelu2":
                    dve.wait_ge(gelu_tanh, p + 1)
                    nc.vector.scalar_tensor_tensor(out=z[:, :], in0=gz[:, :], scalar=1.0, in1=z[:, :],
                                                   op0=ALU.add, op1=ALU.mult).then_inc(gelu_ready, 1)
                elif name == "half2":
                    dve.wait_ge(kept_ready, p + 1)
                    if due(p):
                        dve.wait_ge(kept_spread, p)
                    nc.vector.scalar_tensor_tensor(out=y0[:, :], in0=pf[:, 0:T], scalar=0.5, in1=b2[:, :],
                                                   op0=ALU.mult, op1=ALU.add).then_inc(kept_read, 1)
                elif name == "add2":
                    dve.wait_ge(kept_spread, p + 1)
                    if due(p):
                        dve.wait_ge(attention_added[1], p)
                    nc.vector.scalar_tensor_tensor(out=x2[:, :, :], in0=pf[:, :].rearrange("p (b t) -> p b t", b=NB),
                                                   scalar=tg[:, 1:2], in1=x1[:, :, :],
                                                   op0=ALU.mult, op1=ALU.add).then_inc(mlp0_added, 1)
                elif name == "hidden3":
                    m = OM[k]
                    dve.wait_ge(silu_tanh, OC * p + k + 1)
                    if due(OC * p + k):
                        dve.wait_ge(silu_ready, OC * p + k)
                    nc.vector.scalar_tensor_tensor(out=ga1[0:m, :], in0=th[0:m, k % 2, :], scalar=1.0,
                                                   in1=pf[0:m, 0:T], op0=ALU.add, op1=ALU.mult).then_inc(silu_gate, 1)
                    dve.wait_ge(silu_gate, OC * p + k + 1)
                    if due(p):
                        dve.wait_ge(down_ready, p)
                    nc.vector.tensor_tensor(h1[0:m, k, :], ga1[0:m, :], pf[0:m, T:2 * T], ALU.mult).then_inc(silu_ready, 1)
                elif name == "add3":
                    dve.wait_ge(down_ready, p + 1)
                    nc.vector.scalar_tensor_tensor(out=xnf1[:, :, :], in0=pf[:, :].rearrange("p (b t) -> p b t", b=NB),
                                                   scalar=tgx[:, 1:2], in1=x3[:, :, :],
                                                   op0=ALU.mult, op1=ALU.add).then_inc(mlp1_added, 1)

            program("dve", dve, step)

        @block.gpsimd
        def _(pool):
            nc.gpsimd.memset(mhalf[:, :], -0.5).then_inc(mhalf_set, 1)
            pool.wait_ge(mhalf_set, 1)
            for i, L in enumerate((L0, L1)):
                nc.gpsimd.memset(V[i][:, :, :, L.DH:2 * L.DH], 1.0).then_inc(buffers_set, 1)

            def split(src, hi, lo, sm, n):
                settle(pool, passed_pool)
                nc.gpsimd.tensor_scalar(hi, src, 1.0, None, ALU.mult).then_inc(sm, 1)
                if due(n):
                    pool.wait_ge(sm, n)
                nc.gpsimd.tensor_tensor(lo, src, f32(hi), ALU.subtract).then_inc(sm, 1)

            def step(name, p, k, slot):
                flat = lambda t: t[:, :, :].rearrange("p b t -> p (b t)")
                if name in ("stats0", "stats1", "stats2", "stats3"):
                    i = {"stats0": 0, "stats2": 1, "stats1": 2, "stats3": 3}[name]
                    pool.wait_ge(norm_steps[i], 8 * p + 5)
                    nc.gpsimd.tensor_tensor(rstd[i][:, :], rstd[i][:, :], mhalf[:, :], ALU.pow).then_inc(norm_steps[i], 1)
                elif name == "split0":
                    pool.wait_ge(pair_loaded, 64 * (p + 1))
                    for stored_parts in (q_stored, k_stored):
                        if due(p):
                            pool.wait_ge(stored_parts[0], 16 * p)
                        if due(p - 2):
                            pool.wait_ge(stored_parts[1], 16 * (p - 2))
                    m = flat(mrA)
                    for j, (t, done, hi, lo) in enumerate(((qf, q_read, qhl[:, 0, :], qhl[:, 1, :]), (kf, k_read, khl[:, 0, :], khl[:, 1, :]))):
                        pool.wait_ge(done, p + 1)
                        nc.gpsimd.tensor_tensor(t[:, :], t[:, :], m, ALU.mult).then_inc(split0_done, 1)
                        pool.wait_ge(split0_done, 6 * p + 3 * j + 1)
                        split(t[:, :], hi, lo, split0_done, 6 * p + 3 * j + 2)
                elif name == "values0":
                    pool.wait_ge(v_read, p + 1)
                    if due(L0.U // 4 * p):
                        pool.wait_ge(outputs_ready[0], L0.U // 4 * p)
                    nc.gpsimd.tensor_tensor(V[0][:, :, :, 0:L0.DH], vf[:, :].rearrange("p (j h d) -> p j h d", j=4, h=L0.H),
                                            mc[:, :].unsqueeze(2).unsqueeze(3).to_broadcast([128, 4, L0.H, L0.DH]),
                                            ALU.mult).then_inc(values0_ready, 1)
                elif name == "split1":
                    pool.wait_ge(norm_steps[2], 8 * (p + 1))
                    pool.wait_ge(context1_loaded, 16 * (p + 1))
                    for stored_parts in (q_stored, k_stored):
                        pool.wait_ge(stored_parts[0], 16 * lim(p + 3))
                    split(flat(xnm), qhl[:, 0, :], qhl[:, 1, :], split1_done, 4 * p + 1)
                    split(flat(ctx1), khl[:, 0, :], khl[:, 1, :], split1_done, 4 * p + 3)
                elif name == "keep0":
                    pool.wait_ge(norm_steps[0], 8 * (p + 1))
                    if due(p):
                        pool.wait_ge(attention_added[0], p)
                    settle(pool, passed_pool)
                    nc.gpsimd.tensor_scalar(flat(xr0), flat(xin), 1.0, None, ALU.mult).then_inc(residual_kept, 1)
                elif name == "inner2":
                    pool.wait_ge(gelu_squared, p + 1)
                    settle(pool, passed_pool)
                    nc.gpsimd.tensor_scalar(gz[:, :], gz[:, :], 0.044715, 1.0, ALU.mult, ALU.add).then_inc(gelu_inner, 1)
                    pool.wait_ge(gelu_inner, 2 * p + 1)
                    nc.gpsimd.tensor_tensor(gz[:, :], gz[:, :], z[:, :], ALU.mult).then_inc(gelu_inner, 1)

            program("pool", pool, step)


def kernel(**inputs):
    import numpy as _np
    import concourse.bacc as _bacc
    from concourse import mybir as _mybir
    from concourse.bass_utils import run_bass_kernel_spmd as _run

    v = {k: _np.asarray(x) for k, x in inputs.items()}
    chunks = lambda w, n: _np.pad(w, ((0, n * 128 - w.shape[0]), (0, 0))).reshape(n, 128, -1).transpose(1, 0, 2)
    laid = {
        "x": v["x"], "ctx_2048": v["ctx_2048"],
        "wqT": v["L0_xattn_Wq"].T, "wkT": v["L0_xattn_Wk"].T, "wvT": v["L0_xattn_Wv"].T,
        "bqk": _np.stack([v["L0_xattn_bq"], v["L0_xattn_bk"]], 1), "L0_xattn_bv": v["L0_xattn_bv"],
        "gts": _np.stack([v["g_xattn"][0], v["g_ffn"][0], v["g_xattn"][1], v["g_ffn"][1],
                          v["L1_xattn_gamma"]]).reshape(1, 5),
        "mrow": v["mask_Bx1x2048_fk1"].reshape(NP, N),
        "mcol": v["mask_Bx1x2048_fk1"].reshape(NP, NB * 2, 128).transpose(0, 2, 1),
        "L0_ffn_w_r": v["L0_ffn_w_r"], "br": v["L0_ffn_b_r"].reshape(1, 1),
        "L0_ffn_w1": v["L0_ffn_w1"], "b1c": v["L0_ffn_b1"].reshape(FC, 128).T,
        "L0_ffn_w2": v["L0_ffn_w2"], "L0_ffn_b2": v["L0_ffn_b2"],
        "L1_ffn_lut": v["L1_ffn_lut"],
        "gate_i": chunks(v["L1_ffn_gate_idx"].T, 2), "up_i": chunks(v["L1_ffn_up_idx"].T, 2),
        "down_i": chunks(v["L1_ffn_down_idx"].T, OC),
        "negs": _np.array([[NEG_HI], [NEG_LO]], _np.float32),
        "ident": _np.eye(128, dtype=_np.float32), "tril": _np.tril(_np.ones((128, 128), _np.float32), -1),
        "iota": _np.arange(KEEP, dtype=_np.float32).reshape(1, KEEP),
    }
    nc = _bacc.Bacc("TRN2", target_bir_lowering=False, num_devices=1)
    arrays, aps = {}, {}
    for name, x in laid.items():
        x = _np.ascontiguousarray(x)
        arrays[f"in_{name}"] = x
        aps[name] = nc.dram_tensor(f"in_{name}", x.shape, _mybir.dt.from_np(x.dtype), kind="ExternalInput").ap()
    out = nc.dram_tensor("out", (B, C, T), _mybir.dt.from_np(_np.dtype("float32")), kind="ExternalOutput").ap()
    flamingo_kernel(nc, aps, out)
    r = _run(nc, [arrays], core_ids=[0])
    return r.results[0]["out"]
```
